# Optimizing a Trainium2 kernel written in Bass

```python
import numpy as np
import jax
import jax.numpy as jnp

def _softmax(x, axis=-1):
    return jax.nn.softmax(x, axis=axis)

def _gelu(x):
    return jax.nn.gelu(x, approximate=True)

def _silu(x):
    return jax.nn.silu(x)

def _sigmoid(x):
    return jax.nn.sigmoid(x)

def _layernorm(x, axis=-1, eps=1e-05):
    m = jnp.mean(x, axis=axis, keepdims=True)
    v = jnp.var(x, axis=axis, keepdims=True)
    return (x - m) / jnp.sqrt(v + eps)

def _scatter_add(tgt, idx, src, axis=0):
    return tgt.at[idx].add(src)

def _segment_sum(src, seg, n):
    return jax.ops.segment_sum(src, seg, n)
kernel_name = 'mk_cond_seq_d2_seqx_r8_5299ac'

def setup_inputs(seed: int=0):
    np.random.seed(seed)
    _w = jnp.asarray

    def _rec_inputs():
        import jax
        import jax.numpy as jnp
        _rk = jax.random.key(seed)
        x = 1.648e-05 + 1 * jax.random.normal(jax.random.fold_in(_rk, 1), (2, 512, 144), jnp.float32)
        _lenS = 512 - jax.random.randint(jax.random.fold_in(_rk, 7), (2,), 0, max(1, 512 // 4) + 1, jnp.int32)
        _lenS2 = 512 - jax.random.randint(jax.random.fold_in(_rk, 8), (2,), 0, max(1, 512 // 4) + 1, jnp.int32)
        cond_1152 = 0.00914911 + 1.00357 * jax.random.normal(jax.random.fold_in(_rk, 11), (2, 144), jnp.float32)
        return (x, cond_1152)
    x, cond_1152 = _rec_inputs()

    def _L0_cond_setup():
        import jax, jax.numpy as jnp
        import numpy as np
        B, L, C = (8, 128, 144)
        H = 16
        D = C // H
        FF = int(C * 4.0)
        EPS = 1e-06

        def _layernorm(x):
            mu = jnp.mean(x, axis=-1, keepdims=True)
            var = jnp.mean(jnp.square(x - mu), axis=-1, keepdims=True)
            return (x - mu) * jax.lax.rsqrt(var + EPS)

        def _modulate(x, shift, scale):
            return x * (1.0 + scale) + shift

        def _attention(h, W_qkv, b_qkv, W_proj, b_proj):
            b, l, c = h.shape
            qkv = h @ W_qkv + b_qkv
            qkv = qkv.reshape(b, l, 3, H, D)
            q, k, v = (qkv[:, :, 0], qkv[:, :, 1], qkv[:, :, 2])
            scale = D ** (-0.5)
            scores = jnp.einsum('blhd,bmhd->bhlm', q * scale, k)
            attn = jax.nn.softmax(scores, axis=-1)
            o = jnp.einsum('bhlm,bmhd->blhd', attn, v).reshape(b, l, c)
            return o @ W_proj + b_proj
        key = jax.random.key(seed)
        ks = jax.random.split(key, 12)
        s = 0.02
        return {'x': jax.random.normal(ks[0], (B, L, C), jnp.float32), 'c': jax.random.normal(ks[1], (B, 1, C), jnp.float32), 'W_qkv': jax.random.normal(ks[2], (C, 3 * C), jnp.float32) * s, 'b_qkv': jnp.zeros((3 * C,), jnp.float32), 'W_proj': jax.random.normal(ks[3], (C, C), jnp.float32) * s, 'b_proj': jnp.zeros((C,), jnp.float32), 'W_fc1': jax.random.normal(ks[4], (C, FF), jnp.float32) * s, 'b_fc1': jnp.zeros((FF,), jnp.float32), 'W_fc2': jax.random.normal(ks[5], (FF, C), jnp.float32) * s, 'b_fc2': jnp.zeros((C,), jnp.float32), 'W_ada': jax.random.normal(ks[6], (C, 6 * C), jnp.float32) * s, 'b_ada': jnp.zeros((6 * C,), jnp.float32)}
    _L0_cond_all = _L0_cond_setup()
    _L0_cond_in = {k: v for k, v in _L0_cond_all.items() if k in ('W_qkv', 'b_qkv', 'W_proj', 'b_proj', 'W_fc1', 'b_fc1', 'W_fc2', 'b_fc2', 'W_ada', 'b_ada')}
    del _L0_cond_all

    def _L1_cond_setup():
        import jax, jax.numpy as jnp
        import numpy as np
        B, T, D, H = (64, 32, 144, 16)
        HD = D // H
        EPS = 1e-06

        def _ln(x):
            mu = jnp.mean(x, axis=-1, keepdims=True)
            var = jnp.var(x, axis=-1, keepdims=True)
            return (x - mu) * jax.lax.rsqrt(var + EPS)

        def _modulate(x, shift, scale):
            return x * (1.0 + scale[:, None, :]) + shift[:, None, :]

        def _attn(x, Wq, Wk, Wv, Wp, bp):
            b, t, d = x.shape
            q = (x @ Wq).reshape(b, t, H, HD).transpose(0, 2, 1, 3)
            k = (x @ Wk).reshape(b, t, H, HD).transpose(0, 2, 1, 3)
            v = (x @ Wv).reshape(b, t, H, HD).transpose(0, 2, 1, 3)
            scores = jnp.einsum('bhqd,bhkd->bhqk', q, k) / np.sqrt(HD)
            mask = jnp.triu(jnp.ones((t, t), bool), k=1)
            scores = jnp.where(mask, -jnp.inf, scores)
            w = jax.nn.softmax(scores, axis=-1)
            ctx = jnp.einsum('bhqk,bhkd->bhqd', w, v).transpose(0, 2, 1, 3).reshape(b, t, d)
            return ctx @ Wp + bp

        def _mlp(x, W1, b1, W2, b2):
            return jax.nn.silu(x @ W1 + b1) @ W2 + b2
        key = jax.random.key(seed)
        ks = jax.random.split(key, 12)
        s = lambda fan_in: 1.0 / np.sqrt(fan_in)
        return {'x': jax.random.normal(ks[0], (B, T, D), jnp.float32), 'c': jax.random.normal(ks[1], (B, D), jnp.float32), 'Wq': jax.random.normal(ks[2], (D, D), jnp.float32) * s(D), 'Wk': jax.random.normal(ks[3], (D, D), jnp.float32) * s(D), 'Wv': jax.random.normal(ks[4], (D, D), jnp.float32) * s(D), 'Wp': jax.random.normal(ks[5], (D, D), jnp.float32) * s(D), 'bp': jnp.zeros((D,), jnp.float32), 'W1': jax.random.normal(ks[6], (D, 4 * D), jnp.float32) * s(D), 'b1': jnp.zeros((4 * D,), jnp.float32), 'W2': jax.random.normal(ks[7], (4 * D, D), jnp.float32) * s(4 * D), 'b2': jnp.zeros((D,), jnp.float32), 'Wa': jax.random.normal(ks[8], (D, 6 * D), jnp.float32) * s(D), 'ba': jnp.zeros((6 * D,), jnp.float32)}
    _L1_cond_all = _L1_cond_setup()
    _L1_cond_in = {k: v for k, v in _L1_cond_all.items() if k in ('Wq', 'Wk', 'Wv', 'Wp', 'bp', 'W1', 'b1', 'W2', 'b2', 'Wa', 'ba')}
    del _L1_cond_all
    return {'x': x, 'cond_1152': cond_1152, 'L0_cond_W_qkv': _L0_cond_in['W_qkv'], 'L0_cond_b_qkv': _L0_cond_in['b_qkv'], 'L0_cond_W_proj': _L0_cond_in['W_proj'], 'L0_cond_b_proj': _L0_cond_in['b_proj'], 'L0_cond_W_fc1': _L0_cond_in['W_fc1'], 'L0_cond_b_fc1': _L0_cond_in['b_fc1'], 'L0_cond_W_fc2': _L0_cond_in['W_fc2'], 'L0_cond_b_fc2': _L0_cond_in['b_fc2'], 'L0_cond_W_ada': _L0_cond_in['W_ada'], 'L0_cond_b_ada': _L0_cond_in['b_ada'], 'L1_cond_Wq': _L1_cond_in['Wq'], 'L1_cond_Wk': _L1_cond_in['Wk'], 'L1_cond_Wv': _L1_cond_in['Wv'], 'L1_cond_Wp': _L1_cond_in['Wp'], 'L1_cond_bp': _L1_cond_in['bp'], 'L1_cond_W1': _L1_cond_in['W1'], 'L1_cond_b1': _L1_cond_in['b1'], 'L1_cond_W2': _L1_cond_in['W2'], 'L1_cond_b2': _L1_cond_in['b2'], 'L1_cond_Wa': _L1_cond_in['Wa'], 'L1_cond_ba': _L1_cond_in['ba']}

def reference(x, cond_1152, L0_cond_W_qkv, L0_cond_b_qkv, L0_cond_W_proj, L0_cond_b_proj, L0_cond_W_fc1, L0_cond_b_fc1, L0_cond_W_fc2, L0_cond_b_fc2, L0_cond_W_ada, L0_cond_b_ada, L1_cond_Wq, L1_cond_Wk, L1_cond_Wv, L1_cond_Wp, L1_cond_bp, L1_cond_W1, L1_cond_b1, L1_cond_W2, L1_cond_b2, L1_cond_Wa, L1_cond_ba):
    import jax
    import jax.numpy as jnp

    def _L0_cond_ref(x, c, W_qkv, b_qkv, W_proj, b_proj, W_fc1, b_fc1, W_fc2, b_fc2, W_ada, b_ada):
        import jax, jax.numpy as jnp
        import numpy as np
        B, L, C = (8, 128, 144)
        H = 16
        D = C // H
        FF = int(C * 4.0)
        EPS = 1e-06

        def _layernorm(x):
            mu = jnp.mean(x, axis=-1, keepdims=True)
            var = jnp.mean(jnp.square(x - mu), axis=-1, keepdims=True)
            return (x - mu) * jax.lax.rsqrt(var + EPS)

        def _modulate(x, shift, scale):
            return x * (1.0 + scale) + shift

        def _attention(h, W_qkv, b_qkv, W_proj, b_proj):
            b, l, c = h.shape
            qkv = h @ W_qkv + b_qkv
            qkv = qkv.reshape(b, l, 3, H, D)
            q, k, v = (qkv[:, :, 0], qkv[:, :, 1], qkv[:, :, 2])
            scale = D ** (-0.5)
            scores = jnp.einsum('blhd,bmhd->bhlm', q * scale, k)
            attn = jax.nn.softmax(scores, axis=-1)
            o = jnp.einsum('bhlm,bmhd->blhd', attn, v).reshape(b, l, c)
            return o @ W_proj + b_proj
        ada = jax.nn.silu(c) @ W_ada + b_ada
        shift_msa, scale_msa, gate_msa, shift_mlp, scale_mlp, gate_mlp = jnp.split(ada, 6, axis=-1)
        h = _modulate(_layernorm(x), shift_msa, scale_msa)
        x = x + gate_msa * _attention(h, W_qkv, b_qkv, W_proj, b_proj)
        h = _modulate(_layernorm(x), shift_mlp, scale_mlp)
        mlp = jax.nn.gelu(h @ W_fc1 + b_fc1, approximate=True) @ W_fc2 + b_fc2
        x = x + gate_mlp * mlp
        return x

    def _L1_cond_ref(x, c, Wq, Wk, Wv, Wp, bp, W1, b1, W2, b2, Wa, ba):
        import jax, jax.numpy as jnp
        import numpy as np
        B, T, D, H = (64, 32, 144, 16)
        HD = D // H
        EPS = 1e-06

        def _ln(x):
            mu = jnp.mean(x, axis=-1, keepdims=True)
            var = jnp.var(x, axis=-1, keepdims=True)
            return (x - mu) * jax.lax.rsqrt(var + EPS)

        def _modulate(x, shift, scale):
            return x * (1.0 + scale[:, None, :]) + shift[:, None, :]

        def _attn(x, Wq, Wk, Wv, Wp, bp):
            b, t, d = x.shape
            q = (x @ Wq).reshape(b, t, H, HD).transpose(0, 2, 1, 3)
            k = (x @ Wk).reshape(b, t, H, HD).transpose(0, 2, 1, 3)
            v = (x @ Wv).reshape(b, t, H, HD).transpose(0, 2, 1, 3)
            scores = jnp.einsum('bhqd,bhkd->bhqk', q, k) / np.sqrt(HD)
            mask = jnp.triu(jnp.ones((t, t), bool), k=1)
            scores = jnp.where(mask, -jnp.inf, scores)
            w = jax.nn.softmax(scores, axis=-1)
            ctx = jnp.einsum('bhqk,bhkd->bhqd', w, v).transpose(0, 2, 1, 3).reshape(b, t, d)
            return ctx @ Wp + bp

        def _mlp(x, W1, b1, W2, b2):
            return jax.nn.silu(x @ W1 + b1) @ W2 + b2
        mod = jax.nn.silu(c) @ Wa + ba
        sh_msa, sc_msa, g_msa, sh_mlp, sc_mlp, g_mlp = jnp.split(mod, 6, axis=1)
        x = x + g_msa[:, None, :] * _attn(_modulate(_ln(x), sh_msa, sc_msa), Wq, Wk, Wv, Wp, bp)
        x = x + g_mlp[:, None, :] * _mlp(_modulate(_ln(x), sh_mlp, sc_mlp), W1, b1, W2, b2)
        return x
    x = _L0_cond_ref(x, cond_1152[:, None, :], L0_cond_W_qkv, L0_cond_b_qkv, L0_cond_W_proj, L0_cond_b_proj, L0_cond_W_fc1, L0_cond_b_fc1, L0_cond_W_fc2, L0_cond_b_fc2, L0_cond_W_ada, L0_cond_b_ada)
    x = _L1_cond_ref(x, cond_1152, L1_cond_Wq, L1_cond_Wk, L1_cond_Wv, L1_cond_Wp, L1_cond_bp, L1_cond_W1, L1_cond_b1, L1_cond_W2, L1_cond_b2, L1_cond_Wa, L1_cond_ba)
    return x

_drawn_inputs = setup_inputs


def setup_inputs(seed=0):
    import zlib

    import numpy as np

    out = dict(_drawn_inputs(seed))
    spreads = {'L0_cond_b_qkv': (0.0, 0.8),
     'L0_cond_b_proj': (0.0, 0.413),
     'L0_cond_b_fc1': (0.0, 0.8),
     'L0_cond_b_fc2': (0.0, 0.453),
     'L0_cond_b_ada': (0.0, 0.467),
     'L1_cond_bp': (0.0, 0.361),
     'L1_cond_b1': (0.0, 0.274),
     'L1_cond_b2': (0.0, 0.352),
     'L1_cond_ba': (0.0, 0.1)}
    factors = {'L0_cond_W_qkv': 8.0,
     'L0_cond_W_proj': 8.0,
     'L0_cond_W_fc1': 5.558,
     'L0_cond_W_fc2': 5.206}
    for name, (base, spread) in spreads.items():
        noise = np.random.default_rng([zlib.crc32(name.encode()), seed]).standard_normal(out[name].shape)
        drawn = base * np.exp(spread * noise) if base else spread * noise
        out[name] = jnp.asarray(drawn.astype(out[name].dtype))
    for name, factor in factors.items():
        out[name] = (out[name] * factor).astype(out[name].dtype)
    return out
```

```python
import concourse.bass as bass
import concourse.mybir as mybir
from contextlib import ExitStack

F32 = mybir.dt.float32
BF16 = mybir.dt.bfloat16
ALU = mybir.AluOpType
ACT = mybir.ActivationFunctionType
AX = mybir.AxisListType

P = 128
B, T, C = 2, 512, 144
L = 2
H = 16
D = C // H
FF = 4 * C
NT = T // P
R = C - P
NG = 4
HG = H // NG
QK = 2 * C
QKW = [128, 128, QK - 256]
FW = [128, 128, 128, 128, FF - 512]
NF = len(FW)
VW = 32
EPS = 1e-6
SCALE = float(D) ** -0.5
NEG = -1e30
GELU_C = 0.7978845608028654
GELU_A = 0.044715

QPART = [0, 0, 1, 0, 2, 1]
KPART = [0, 1, 0, 2, 0, 1]
MROW = len(QPART) * D
KROWS = 96
LEAD = 12

SH, SC, GA = 0, 1, 2


def head_items(l, b):
    return ([("stats", l, b, 0), ("norm", l, b, 0), ("hT", l, b, 0, 0), ("hT", l, b, 0, 1)]
            + [("qk", l, b, c) for c in range(3)] + [("v", l, b, i) for i in range(2)])


def tail_items(l, b):
    items = [("aT", l, b, 0), ("aT", l, b, 1), ("proj", l, b, 0), ("proj", l, b, 1),
             ("stats", l, b, 1), ("norm", l, b, 1), ("hT", l, b, 1, 0), ("hT", l, b, 1, 1)]
    for c in range(NF + 2):
        if c < NF:
            items.append(("fc1", l, b, c))
        if c >= 1 and c - 1 < NF:
            items.append(("tanh", l, b, c - 1))
        if c >= 2:
            items.append(("gate", l, b, c - 2))
    return items + [("fc2", l, b, 0), ("fc2", l, b, 1)]


def make_schedule():
    steps = L * B * NG * 8
    out = [("stats", 0, 0, 0), ("ada",)] + [i for i in head_items(0, 0) if i[0] != "stats"]
    for n in range(2 * LEAD):
        out.append(("rowmax", n // 16, n % 16))
        if n % 16 == 15:
            out += [("msplit", n // 16), ("mT", n // 16)]
    behind = {0: head_items(0, 1), 1: tail_items(0, 0) + head_items(1, 0),
              2: tail_items(0, 1) + head_items(1, 1), 3: tail_items(1, 0)}
    later = {}
    for s in range(steps):
        p, r = divmod(s, 8 * NG)
        if r == 0:
            todo = list(behind[p])
            rate = len(todo) / (8 * NG - LEAD)
            done = 0
        out.append(("probs", s // 8, s % 8))
        for n in (2 * (s + LEAD), 2 * (s + LEAD) + 1):
            if n < 2 * steps:
                out.append(("rowmax", n // 16, n % 16))
                if n % 16 == 15:
                    later.setdefault(s + 1, []).append(("msplit", n // 16))
                    later.setdefault(s + 2, []).append(("mT", n // 16))
        out += later.pop(s, [])
        if r >= 2 and todo:
            want = int((r - 1) * rate * 1.15 + 0.999)
            while done < want and todo:
                out.append(todo.pop(0))
                done += 1
        if s % 2 == 0 and s:
            out.append(("pv", (s // 2 - 1) // 4, (s // 2 - 1) % 4))
        if s % 8 == 0 and s:
            out.append(("oT", s // 8 - 1))
        if s % 8 == 1 and s > 8:
            out.append(("o", s // 8 - 1))
        if r == 8 * NG - 1:
            out += todo
    last = steps // 8 - 1
    out += [("pv", last, 3), ("oT", last), ("o", last)]
    return out + tail_items(1, 1)


SCHEDULE = make_schedule()
SHARED = ("hT", "qk", "v", "aT", "proj", "fc1", "fc2", "mT", "o")


def ordinals(kinds):
    n, out = 0, {}
    for item in SCHEDULE:
        if item[0] in kinds:
            n += 1
            out[item] = n
    return out


def two_block_kernel(nc, a, out):
    ctx = ExitStack()

    def sb(name, shape, dt=F32):
        return ctx.enter_context(nc.sbuf_tensor(name, shape, dt))

    def ps(name, shape):
        return ctx.enter_context(nc.psum_tensor(name, shape, F32))

    def sem(name):
        return ctx.enter_context(nc.semaphore(name))

    with ctx:
        ident = sb("ident", [P, P])
        identb = sb("identb", [P, P], BF16)
        mask_qk = sb("mask_qk", [P, P], BF16)
        mask_kq = sb("mask_kq", [P, P], BF16)
        onesb = sb("onesb", [P, T], BF16)
        zerosb = sb("zerosb", [P, T], BF16)
        w_qkv = [sb(f"w_qkv{l}", [P, 3 * C]) for l in range(L)]
        w_qkv_r = [sb(f"w_qkv_r{l}", [R + 1, 3 * C]) for l in range(L)]
        w_proj = [sb(f"w_proj{l}", [P, C]) for l in range(L)]
        w_proj_r = [sb(f"w_proj_r{l}", [R + 1, C]) for l in range(L)]
        w_fc1 = [sb(f"w_fc1{l}", [P, FF]) for l in range(L)]
        w_fc1_r = [sb(f"w_fc1_r{l}", [R + 1, FF]) for l in range(L)]
        w_fc2 = [sb(f"w_fc2{l}", [P, NF, C]) for l in range(L)]
        g_proj = [[sb(f"g_proj{l}{b}", [P, C]) for b in range(B)] for l in range(L)]
        g_proj_r = [[sb(f"g_proj_r{l}{b}", [R + 1, C]) for b in range(B)] for l in range(L)]
        g_fc2 = [[sb(f"g_fc2{l}{b}", [P, NF, C]) for b in range(B)] for l in range(L)]
        cond = sb("cond", [P, 4, B])
        cond_r = sb("cond_r", [R + 1, 4, B])
        ada_row = [sb(f"ada_row{l}", [B, 6 * C]) for l in range(L)]
        pick = sb("pick", [B, B, P])
        mod = [sb(f"mod{l}", [P, 2, 2, B]) for l in range(L)]
        mod_r = [sb(f"mod_r{l}", [R, 2, 2, B]) for l in range(L)]
        X = [sb(f"X{b}", [P, NT, C]) for b in range(B)]
        stat = [sb(f"stat{b}", [P, NT, 6]) for b in range(B)]
        mean = [sb(f"mean{b}", [P, NT, 2]) for b in range(B)]
        veps = [sb(f"veps{b}", [P, NT]) for b in range(B)]
        rstd = [sb(f"rstd{b}", [P, NT]) for b in range(B)]
        half = sb("half", [P, NT])
        hn = [sb(f"hn{b}", [P, NT, C]) for b in range(B)]
        hT = [sb(f"hT{b}", [P, T]) for b in range(B)]
        hT_r = [sb(f"hT_r{b}", [R + 1, T]) for b in range(B)]
        parts = sb("parts", [P, 3, 3, T], BF16)
        rest = sb("rest", [P, T])
        QS = [sb(f"QS{b}", [P, H, T], BF16) for b in range(B)]
        KS = [sb(f"KS{b}", [P, H, T], BF16) for b in range(B)]
        V = [sb(f"V{b}", [P, NT, H, VW]) for b in range(B)]
        probs = sb("probs", [P, 2, HG, T])
        negm = sb("negm", [P, 2, NT, HG])
        mrest = sb("mrest", [P, NT, HG])
        msp = sb("msp", [P, NT, 3, HG], BF16)
        mT = sb("mT", [3 * HG, 2, T], BF16)
        OT = sb("OT", [P, T])
        rden = sb("rden", [P, NT, HG])
        at = [sb(f"at{b}", [P, NT, C]) for b in range(B)]
        aT = sb("aT", [P, T])
        aT_r = sb("aT_r", [R + 1, T])
        xh = sb("xh", [P, NF, T])
        U = sb("U", [P, NF, T])
        wide = probs[:, :, :, :].rearrange("p k h t -> p (k h t)")
        w_ada = [xh[:, :, :].rearrange("p c t -> p (c t)")[:, l * 6 * C:(l + 1) * 6 * C] for l in range(L)]
        w_ada_r = [wide[0:R + 1, l * 6 * C:(l + 1) * 6 * C] for l in range(L)]
        gates = [[U[:, l * B + b, 0:2 * C].rearrange("p (k c) -> p k c", k=2) for b in range(B)] for l in range(L)]

        SM = [ps(f"SM{i}", [P, T]) for i in range(2)]
        ST = [ps(f"ST{i}", [P, 2, T]) for i in range(2)]
        OB = ps("OB", [P, T])
        BG = ps("BG", [P, T])
        BGm = BG[:, :].bitcast(BF16)[:, 0:T]

        scratch = nc.dram_tensor("qk_parts", [L, B, 3, QK, T], BF16, kind="Internal").ap()

        cond_in = sem("cond_in")
        ada_in = [sem(f"ada_in{l}") for l in range(L)]
        x_in = [sem(f"x_in{b}") for b in range(B)]
        qkv_in = [sem(f"qkv_in{l}") for l in range(L)]
        proj_in = [sem(f"proj_in{l}") for l in range(L)]
        fc1_in = [sem(f"fc1_in{l}") for l in range(L)]
        filled = sem("filled")
        q_zeroed = sem("q_zeroed")
        k_zeroed = sem("k_zeroed")
        consts = sem("consts")
        pool_step = sem("pool_step")
        dve_step = sem("dve_step")
        th_ready = sem("th_ready")
        silu_ready = sem("silu_ready")
        ada_full = sem("ada_full")
        row_ready = sem("row_ready")
        col_full = sem("col_full")
        mod_ready = sem("mod_ready")
        gate_full = sem("gate_full")
        gates_ready = sem("gates_ready")
        gated = sem("gated")
        stats_ready = sem("stats_ready")
        rstd_ready = sem("rstd_ready")
        normed = sem("normed")
        shared_full = sem("shared_full")
        shared_free = sem("shared_free")
        high_ready = sem("high_ready")
        parts_ready = sem("parts_ready")
        parts_out = sem("parts_out")
        stacked = [[sem(f"stacked{p}{i}") for i in range(2)] for p in range(L * B)]
        ones_in = sem("ones_in")
        rowmax_full = sem("rowmax_full")
        rowmax_done = sem("rowmax_done")
        msplit_ready = sem("msplit_ready")
        m_in = [sem(f"m_in{i}") for i in range(2)]
        scores_ready = sem("scores_ready")
        probs_ready = sem("probs_ready")
        pv_done = sem("pv_done")
        o_ready = sem("o_ready")
        u_ready = sem("u_ready")
        t_ready = sem("t_ready")
        g_ready = sem("g_ready")
        x_ready = sem("x_ready")
        stored = sem("stored")

        SHARE = ordinals(SHARED)
        FREE = ordinals(tuple(k for k in SHARED if k not in ("proj", "fc2")))
        STATS = ordinals(("stats",))
        NORM = ordinals(("norm",))
        QKN = ordinals(("qk",))
        MAXN = ordinals(("rowmax",))
        MSPL = ordinals(("msplit",))
        PROB = ordinals(("probs",))
        PVN = ordinals(("pv",))
        ON = ordinals(("oT",))
        GATE = ordinals(("gate",))
        TANH = ordinals(("tanh",))
        XN = ordinals(("proj", "fc2"))
        GELU_U = {i: n for n, i in enumerate((i for i in SCHEDULE if i[0] == "fc1" and i[1] == 0), 1)}
        NSTACK = len(QPART) * 2

        def lb(g):
            return g // (B * NG), g // NG % B, g % NG * HG

        def keys_of(l, qt):
            return (qt + 1) * P if l else T

        def first_query(l, kt):
            return kt * P if l else 0

        block = ctx.enter_context(nc.Block())

        @block.sync
        def _(sp):
            sp.dma_start(cond[:, 0, :], a["cond_1152"][0:P]).then_inc(cond_in, 16)
            sp.dma_start(cond_r[0:R, 0, :], a["cond_1152"][P:C]).then_inc(cond_in, 16)
            ada = [("L0_cond_W_ada", "L0_cond_b_ada"), ("L1_cond_Wa", "L1_cond_ba")]

            def load(dst, dst_r, w, bias, s):
                sp.dma_start(dst, w[0:P, :]).then_inc(s, 16)
                sp.dma_start(dst_r[0:R], w[P:C, :]).then_inc(s, 16)
                if bias is not None:
                    sp.dma_start(dst_r[R:R + 1], bias.rearrange("(a n) -> a n", a=1)).then_inc(s, 16)

            def load_x(b):
                sp.dma_start(X[b][:, :, :], a["x"][b].rearrange("(t p) c -> p t c", p=P)).then_inc(x_in[b], 16)

            load(w_ada[0], w_ada_r[0], a[ada[0][0]], a[ada[0][1]], ada_in[0])
            load_x(0)
            load(w_qkv[0][:, :], w_qkv_r[0], a["L0_cond_W_qkv"], a["L0_cond_b_qkv"], qkv_in[0])
            load_x(1)
            load(w_ada[1], w_ada_r[1], a[ada[1][0]], a[ada[1][1]], ada_in[1])
            sp.wait_ge(filled, 1)
            names = [("L0_cond_W_proj", "L0_cond_b_proj", "L0_cond_W_fc1", "L0_cond_b_fc1",
                      "L0_cond_W_fc2", "L0_cond_b_fc2"),
                     ("L1_cond_Wp", "L1_cond_bp", "L1_cond_W1", "L1_cond_b1", "L1_cond_W2", "L1_cond_b2")]
            for l, (wp, bp, w1, b1, w2, b2) in enumerate(names):
                load(w_proj[l][:, :], w_proj_r[l], a[wp], a[bp], proj_in[l])
                sp.dma_start(w_fc2[l][:, 0:4, :], a[w2][0:4 * P, :].rearrange("(c p) n -> p c n", p=P)).then_inc(proj_in[l], 16)
                sp.dma_start(w_fc2[l][0:FW[4], 4, :], a[w2][4 * P:FF, :]).then_inc(proj_in[l], 16)
                sp.dma_start(w_fc2[l][FW[4]:FW[4] + 1, 4, :], a[b2].rearrange("(a n) -> a n", a=1)).then_inc(proj_in[l], 16)
                load(w_fc1[l][:, :], w_fc1_r[l], a[w1], a[b1], fc1_in[l])
            for i, w in enumerate(("L1_cond_Wq", "L1_cond_Wk", "L1_cond_Wv")):
                sp.dma_start(w_qkv[1][:, i * C:(i + 1) * C], a[w][0:P, :]).then_inc(qkv_in[1], 16)
                sp.dma_start(w_qkv_r[1][0:R, i * C:(i + 1) * C], a[w][P:C, :]).then_inc(qkv_in[1], 16)

            for kind, *args in SCHEDULE:
                if kind == "qk":
                    l, b, c = args
                    sp.wait_ge(parts_ready, QKN[("qk", l, b, c)])
                    w = QKW[c]
                    sp.dma_start(scratch[l, b, :, c * P:c * P + w, :].rearrange("s r t -> r s t"),
                                 parts[0:w, c, :, :]).then_inc(parts_out, 16)
                    if c < 2:
                        continue
                    sp.wait_ge(parts_out, 16 * QKN[("qk", l, b, c)])
                    if l == 0:
                        sp.wait_ge(q_zeroed, b + 1)
                        sp.wait_ge(k_zeroed, b + 1)
                        sp.dma_start(KS[b][MROW:MROW + 3, :, :],
                                     onesb[0:3, None, :].to_broadcast([3, H, T])).then_inc(ones_in, 16)
                    if l:
                        sp.wait_ge(scores_ready, PROB[("probs", (b + 1) * NG - 1, 7)])
                    for i, (h0, h1) in enumerate(((0, HG), (HG, H))):
                        done = stacked[l * B + b][i]
                        for n in range(len(QPART)):
                            for dst, part, first in ((QS[b], QPART[n], 0), (KS[b], KPART[n], C)):
                                src = scratch[l, b, part, first:first + C, :].rearrange("(h d) t -> d h t", d=D)
                                sp.dma_start(dst[n * D:(n + 1) * D, h0:h1, :], src[:, h0:h1, :]).then_inc(done, 16)
                        if l:
                            sp.dma_start(QS[b][MROW:MROW + 3, h0:h1, :],
                                         zerosb[0:3, None, :].to_broadcast([3, h1 - h0, T])).then_inc(done, 16)
                elif kind == "mT":
                    g, = args
                    l, b, h = lb(g)
                    sp.wait_ge(shared_free, FREE[("mT", g)])
                    for i in range(3):
                        sp.dma_start(QS[b][MROW + i:MROW + i + 1, h:h + HG, :],
                                     mT[i * HG:(i + 1) * HG, g % 2, :]).then_inc(m_in[g % 2], 16)
                elif kind == "fc2" and args[0] == L - 1:
                    l, b, i = args
                    sp.wait_ge(x_ready, XN[("fc2", l, b, i)])
                    sp.dma_start(out[b, 2 * i * P:2 * (i + 1) * P, :].rearrange("(t p) c -> p t c", p=P),
                                 X[b][:, 2 * i:2 * i + 2, :]).then_inc(stored, 16)
            sp.wait_ge(ones_in, 32)
            sp.wait_ge(stored, 16 * 2 * B)

        @block.gpsimd
        def _(pool):
            chain = [0]

            def link(ins):
                chain[0] += 1
                ins.then_inc(pool_step, 1)
                pool.wait_ge(pool_step, chain[0])

            nc.gpsimd.memset(ident[:, :], 0.0)
            nc.gpsimd.memset(identb[:, :], 0.0)
            nc.gpsimd.memset(mask_qk[:, :], 0.0)
            link(nc.gpsimd.memset(mask_kq[:, :], 0.0))
            nc.gpsimd.affine_select(out=ident[:, :], in_=ident[:, :], compare_op=ALU.not_equal, fill=1.0,
                                    base=0, pattern=[[-1, P]], channel_multiplier=1)
            nc.gpsimd.affine_select(out=identb[:, :], in_=identb[:, :], compare_op=ALU.not_equal, fill=1.0,
                                    base=0, pattern=[[-1, P]], channel_multiplier=1)
            nc.gpsimd.memset(half[:, :], -0.5).then_inc(consts, 1)
            nc.gpsimd.affine_select(out=mask_qk[:, :], in_=mask_qk[:, :], compare_op=ALU.is_ge, fill=NEG,
                                    base=0, pattern=[[-1, P]], channel_multiplier=1)
            nc.gpsimd.affine_select(out=mask_kq[:, :], in_=mask_kq[:, :], compare_op=ALU.is_ge, fill=NEG,
                                    base=0, pattern=[[1, P]], channel_multiplier=-1).then_inc(consts, 1)

            for b in range(B):
                nc.gpsimd.memset(KS[b][0:KROWS, :, :].bitcast(mybir.dt.uint32), 0).then_inc(k_zeroed, 1)

            def gate_weights(l, b):
                pool.wait_ge(gates_ready, l * B + b + 1)
                if b == 0:
                    pool.wait_ge(proj_in[l], 16 * 6)
                g = gates[l][b]
                nc.gpsimd.tensor_tensor(g_proj[l][b][:, :], w_proj[l][:, :], g[:, 0, :], ALU.mult)
                nc.gpsimd.tensor_tensor(g_proj_r[l][b][:, :], w_proj_r[l][:, :], g[0:R + 1, 0, :], ALU.mult)
                for c in range(NF):
                    w = FW[c] + (c == NF - 1)
                    last = nc.gpsimd.tensor_tensor(g_fc2[l][b][0:w, c, :], w_fc2[l][0:w, c, :], g[0:w, 1, :], ALU.mult)
                last.then_inc(gated, 1)

            for kind, *args in SCHEDULE:
                if kind == "stats":
                    l, b, k = args
                    n = STATS[("stats", l, b, k)]
                    pool.wait_ge(stats_ready, n)
                    if n == 1:
                        pool.wait_ge(consts, 1)
                    nc.gpsimd.tensor_tensor(rstd[b][:, :], veps[b][:, :], half[:, :], ALU.pow).then_inc(rstd_ready, 1)
                elif kind == "msplit":
                    g, = args
                    pool.wait_ge(rowmax_done, 16 * (g + 1))
                    if g:
                        pool.wait_ge(shared_full, SHARE[("mT", g - 1)])
                    m = negm[:, g % 2, :, :]
                    link(nc.gpsimd.tensor_copy(msp[:, :, 0, :], m))
                    link(nc.gpsimd.tensor_tensor(mrest[:, :, :], m, msp[:, :, 0, :], ALU.subtract))
                    link(nc.gpsimd.tensor_copy(msp[:, :, 1, :], mrest[:, :, :]))
                    nc.gpsimd.tensor_tensor(msp[:, :, 2, :], mrest[:, :, :], msp[:, :, 1, :],
                                            ALU.subtract).then_inc(msplit_ready, 1)
                    if g < L * B:
                        gate_weights(g // B, g % B)

        @block.scalar
        def _(act):
            act.wait_ge(silu_ready, 1)
            nc.scalar.activation(cond[:, 2, :], cond[:, 1, :], ACT.Tanh)
            nc.scalar.activation(cond_r[0:R, 2, :], cond_r[0:R, 1, :], ACT.Tanh).then_inc(th_ready, 1)

            for kind, *args in SCHEDULE:
                item = (kind, *args)
                if kind == "hT":
                    l, b, k, r = args
                    act.wait_ge(shared_full, SHARE[item])
                    act.wait_ge(mod_ready, l + 1)
                    m = (mod_r if r else mod)[l]
                    dst = hT_r[b][0:R, :] if r else hT[b][:, :]
                    n = R if r else P
                    nc.scalar.activation(dst, BG[0:n, :], ACT.Identity, scale=m[:, k, SC, b:b + 1],
                                         bias=m[:, k, SH, b:b + 1]).then_inc(shared_free, 1)
                elif kind == "qk":
                    l, b, c = args
                    act.wait_ge(shared_full, SHARE[item])
                    if QKN[item] > 3:
                        act.wait_ge(parts_out, 16 * 3 * ((QKN[item] - 1) // 3))
                    w = QKW[c]
                    nc.scalar.activation(parts[0:w, c, 0, :], BG[0:w, :], ACT.Copy).then_inc(high_ready, 1)
                elif kind == "mT":
                    g, = args
                    act.wait_ge(shared_full, SHARE[item])
                    if g >= 2:
                        act.wait_ge(m_in[g % 2], 48 * (g // 2))
                    nc.scalar.activation(mT[:, g % 2, :], BGm[0:3 * HG, :], ACT.Copy).then_inc(shared_free, 1)
                elif kind == "probs":
                    g, u = args
                    l, b, h = lb(g)
                    kt, pair = divmod(u, 2)
                    n = PROB[item]
                    act.wait_ge(scores_ready, n)
                    if n > 4:
                        act.wait_ge(pv_done, (n - 5) // 2 + 1)
                    q0 = first_query(l, kt)
                    nc.scalar.activation(probs[:, kt % 2, 2 * pair:2 * pair + 2, q0:T], ST[(n - 1) % 2][:, :, q0:T],
                                         ACT.Exp, scale=SCALE).then_inc(probs_ready, 1)
                elif kind == "oT":
                    g, = args
                    act.wait_ge(pv_done, PVN[("pv", g, 3)])
                    if g:
                        act.wait_ge(shared_full, SHARE[("o", g - 1)])
                    nc.scalar.activation(OT[:, :], OB[:, :], ACT.Copy).then_inc(o_ready, 1)
                elif kind == "aT":
                    l, b, r = args
                    act.wait_ge(shared_full, SHARE[item])
                    dst, n = (aT_r[0:R, :], R) if r else (aT[:, :], P)
                    nc.scalar.activation(dst, BG[0:n, :], ACT.Copy).then_inc(shared_free, 1)
                elif kind == "fc1":
                    l, b, c = args
                    act.wait_ge(shared_full, SHARE[item])
                    before = ("gate", *((l, 0) if b else (l - 1, 1)), c)
                    if (l, b, c) == (0, 0, 0):
                        act.wait_ge(gated, L * B)
                    if before in GATE:
                        act.wait_ge(g_ready, GATE[before])
                    w = FW[c]
                    nc.scalar.activation(U[0:w, c, :], BG[0:w, :], ACT.Tanh if l else ACT.Square, scale=0.5)
                    nc.scalar.activation(xh[0:w, c, :], BG[0:w, :], ACT.Copy, scale=0.5).then_inc(shared_free, 1)
                elif kind == "tanh" and args[0] == 0:
                    l, b, c = args
                    act.wait_ge(u_ready, GELU_U[("fc1", l, b, c)])
                    w = FW[c]
                    nc.scalar.activation(U[0:w, c, :], U[0:w, c, :], ACT.Tanh).then_inc(t_ready, 1)

        @block.vector
        def _(dve):
            chain = [0]

            def link(ins):
                chain[0] += 1
                ins.then_inc(dve_step, 1)
                dve.wait_ge(dve_step, chain[0])

            nc.vector.memset(onesb[:, :], 1.0)
            nc.vector.memset(zerosb[:, :], 0.0)
            nc.vector.memset(w_qkv_r[1][:, :], 0.0)
            nc.vector.memset(cond_r[:, 3, :], 1.0)
            for b in range(B):
                nc.vector.memset(hT_r[b][:, :], 1.0)
            nc.vector.memset(aT_r[:, :], 1.0)
            nc.vector.memset(U[FW[4]:FW[4] + 1, 4, :], 1.0).then_inc(filled, 1)
            dve.wait_ge(cond_in, 32)
            nc.vector.tensor_scalar(cond[:, 1, :], cond[:, 0, :], 0.5, None, ALU.mult)
            nc.vector.tensor_scalar(cond_r[0:R, 1, :], cond_r[0:R, 0, :], 0.5, None, ALU.mult).then_inc(silu_ready, 1)

            def make_ada():
                dve.wait_ge(th_ready, 1)
                dve.wait_ge(silu_ready, 1)
                nc.vector.scalar_tensor_tensor(cond[:, 3, :], cond[:, 2, :], 1.0, cond[:, 1, :], ALU.add, ALU.mult)
                nc.vector.scalar_tensor_tensor(cond_r[0:R, 3, :], cond_r[0:R, 2, :], 1.0, cond_r[0:R, 1, :],
                                               ALU.add, ALU.mult).then_inc(silu_ready, 1)
                dve.wait_ge(consts, 1)
                for b in range(B):
                    nc.vector.tensor_copy(pick[:, b, :], ident[0:B, b:b + 1].to_broadcast([B, P]))
                for l in range(L):
                    dve.wait_ge(ada_full, l + 1)
                    nc.vector.tensor_copy(ada_row[l][:, :].rearrange("b (k n) -> b k n", k=2),
                                          ST[l][0:B, :, 0:3 * C]).then_inc(row_ready, 1)
                for l in range(L):
                    dve.wait_ge(col_full, l + 1)
                    for dst, n, at0 in ((mod[l], P, 0), (mod_r[l], R, 8)):
                        src = SM[l][0:n, at0:at0 + 8].rearrange("p (k s b) -> p k s b", k=2, s=2)
                        nc.vector.tensor_copy(dst[:, :, SH, :], src[:, :, 0, :])
                        last = nc.vector.tensor_scalar(dst[:, :, SC, :], src[:, :, 1, :], 1.0, None, ALU.add)
                    last.then_inc(mod_ready, 1)
                for l in range(L):
                    for b in range(B):
                        dve.wait_ge(gate_full, l * B + b + 1)
                        nc.vector.tensor_copy(gates[l][b][:, :, :], ST[l][:, b, 0:2 * C].rearrange("p (k c) -> p k c", k=2)
                                              ).then_inc(gates_ready, 1)

            for kind, *args in SCHEDULE:
                item = (kind, *args)
                if kind == "ada":
                    make_ada()
                    for b in range(B):
                        last = nc.vector.memset(V[b][:, :, :, :], 0.0)
                    link(last)
                    for b in range(B):
                        last = nc.vector.memset(V[b][:, :, :, D:D + 1], 1.0)
                    link(last)
                elif kind == "stats":
                    l, b, k = args
                    if (l, k) == (0, 0):
                        dve.wait_ge(x_in[b], 16)
                    else:
                        dve.wait_ge(x_ready, XN[("proj", l, b, 1) if k else ("fc2", l - 1, b, 1)])
                    for t in range(NT):
                        ins = nc.vector.bn_stats(stat[b][:, t, :], X[b][:, t, :])
                    link(ins)
                    for t in range(NT):
                        ins = nc.vector.bn_aggr(mean[b][:, t, :], stat[b][:, t, :])
                    link(ins)
                    nc.vector.tensor_scalar(veps[b][:, :], mean[b][:, :, 1], EPS, None, ALU.add).then_inc(stats_ready, 1)
                    if (l, k) == (0, 0):
                        nc.vector.memset(QS[b][0:KROWS, :, :].bitcast(mybir.dt.uint32), 0).then_inc(q_zeroed, 1)
                elif kind == "norm":
                    l, b, k = args
                    dve.wait_ge(rstd_ready, STATS[("stats", l, b, k)])
                    dve.wait_ge(stats_ready, STATS[("stats", l, b, k)])
                    if (l, k) != (0, 0):
                        dve.wait_ge(shared_full, SHARE[("hT", *((l, b, 0) if k else (l - 1, b, 1)), 1)])
                    for t in range(NT):
                        ins = nc.vector.tensor_scalar(hn[b][:, t, :], X[b][:, t, :], mean[b][:, t, 0:1],
                                                      rstd[b][:, t:t + 1], ALU.subtract, ALU.mult)
                    ins.then_inc(normed, 1)
                elif kind == "qk":
                    l, b, c = args
                    w = QKW[c]
                    dve.wait_ge(high_ready, QKN[item])
                    hi, mid, lo = (parts[0:w, c, i, :] for i in range(3))
                    nc.vector.tensor_tensor(rest[0:w, :], BG[0:w, :], hi, ALU.subtract).then_inc(shared_free, 1)
                    dve.wait_ge(shared_free, FREE[item])
                    link(nc.vector.tensor_copy(mid, rest[0:w, :]))
                    nc.vector.tensor_tensor(lo, rest[0:w, :], mid, ALU.subtract).then_inc(parts_ready, 1)
                    dve.wait_ge(parts_ready, QKN[item])
                elif kind == "v":
                    l, b, i = args
                    dve.wait_ge(shared_full, SHARE[item])
                    if l:
                        dve.wait_ge(pv_done, PVN[("pv", (b + 1) * NG - 1, 3)])
                    nc.vector.tensor_copy(V[b][:, 2 * i:2 * i + 2, :, 0:D],
                                          BG[:, 0:2 * C].rearrange("p (t h d) -> p t h d", t=2, h=H)
                                          ).then_inc(shared_free, 1)
                elif kind == "rowmax":
                    g, u = args
                    l, b, h = lb(g)
                    j, qt = divmod(u, NT)
                    n = MAXN[item]
                    dve.wait_ge(rowmax_full, n)
                    if g >= 2 and u == 0:
                        dve.wait_ge(msplit_ready, g - 1)
                    nc.vector.tensor_reduce(negm[:, g % 2, qt, j:j + 1], SM[(n - 1) % 2][:, 0:keys_of(l, qt)],
                                            AX.X, ALU.max, negate=True).then_inc(rowmax_done, 1)
                elif kind == "o":
                    g, = args
                    l, b, h = lb(g)
                    dve.wait_ge(shared_full, SHARE[item])
                    if l and g % NG == 0:
                        dve.wait_ge(shared_full, SHARE[("aT", l - 1, b, 1)])
                    o = BG[:, :].rearrange("p (t j c) -> p t j c", t=NT, j=HG)
                    link(nc.vector.reciprocal(rden[:, :, :], o[:, :, :, D]))
                    nc.vector.tensor_tensor(at[b][:, :, h * D:(h + HG) * D].rearrange("p t (j d) -> p t j d", j=HG),
                                            o[:, :, :, 0:D], rden[:, :, :, None].to_broadcast([P, NT, HG, D]),
                                            ALU.mult).then_inc(shared_free, 1)
                elif kind in ("proj", "fc2"):
                    l, b, i = args
                    dve.wait_ge(shared_full, SHARE[item])
                    if XN[item] > 1:
                        dve.wait_ge(x_ready, XN[item] - 1)
                    x = X[b][:, 2 * i:2 * i + 2, :]
                    ins = nc.vector.tensor_tensor(x, x, BG[:, 0:2 * C].rearrange("p (t c) -> p t c", t=2), ALU.add)
                    ins.then_inc(x_ready, 1)
                elif kind == "fc1" and args[0] == 0:
                    l, b, c = args
                    w = FW[c]
                    dve.wait_ge(shared_free, FREE[item])
                    u = U[0:w, c, :]
                    link(nc.vector.tensor_scalar(u, u, 8 * GELU_C * GELU_A, 2 * GELU_C, ALU.mult, ALU.add))
                    nc.vector.tensor_tensor(u, u, xh[0:w, c, :], ALU.mult).then_inc(u_ready, 1)
                elif kind == "gate":
                    l, b, c = args
                    w = FW[c]
                    if l == 0:
                        dve.wait_ge(t_ready, GELU_U[("fc1", l, b, c)])
                    dve.wait_ge(shared_free, FREE[("fc1", l, b, c)])
                    u = U[0:w, c, :]
                    nc.vector.scalar_tensor_tensor(u, u, 1.0, xh[0:w, c, :], ALU.add, ALU.mult).then_inc(g_ready, 1)

        @block.tensor
        def _(pe):
            pe.wait_ge(consts, 2)

            def make_ada():
                pe.wait_ge(silu_ready, 2)
                for l in range(L):
                    pe.wait_ge(ada_in[l], 48)
                    for k in range(2):
                        cols = slice(k * 3 * C, (k + 1) * 3 * C)
                        nc.tensor.matmul(ST[l][0:B, k, 0:3 * C], cond[:, 3, :], w_ada[l][:, cols], start=True, stop=False)
                        ins = nc.tensor.matmul(ST[l][0:B, k, 0:3 * C], cond_r[:, 3, :], w_ada_r[l][:, cols],
                                               start=False, stop=True)
                    ins.then_inc(ada_full, 1)
                for l in range(L):
                    pe.wait_ge(row_ready, l + 1)
                    for k in range(2):
                        for s in range(2):
                            at0 = (k * 2 + s) * B
                            c0 = (3 * k + s) * C
                            nc.tensor.transpose(SM[l][:, at0:at0 + B], ada_row[l][:, c0:c0 + P], ident[0:B, 0:B])
                            ins = nc.tensor.transpose(SM[l][0:R, 8 + at0:8 + at0 + B], ada_row[l][:, c0 + P:c0 + C],
                                                      ident[0:B, 0:B])
                    ins.then_inc(col_full, 1)
                for l in range(L):
                    for b in range(B):
                        for k in range(2):
                            c0 = (3 * k + GA) * C
                            ins = nc.tensor.matmul(ST[l][:, b, k * C:(k + 1) * C], pick[:, b, :], ada_row[l][:, c0:c0 + C],
                                                   start=True, stop=True)
                        ins.then_inc(gate_full, 1)

            last_filled = None
            for kind, *args in SCHEDULE:
                item = (kind, *args)
                if item in SHARE:
                    if last_filled in FREE:
                        pe.wait_ge(shared_free, FREE[last_filled])
                    elif last_filled:
                        pe.wait_ge(x_ready, XN[last_filled])
                    last_filled = item
                if kind == "ada":
                    make_ada()
                elif kind == "hT":
                    l, b, k, r = args
                    pe.wait_ge(normed, NORM[("norm", l, b, k)])
                    for t in range(NT):
                        src = hn[b][:, t, P:C] if r else hn[b][:, t, 0:P]
                        n = R if r else P
                        ins = nc.tensor.transpose(BG[0:n, t * P:(t + 1) * P], src, ident[:, :])
                    ins.then_inc(shared_full, 1)
                elif kind == "qk":
                    l, b, c = args
                    pe.wait_ge(qkv_in[l], 96 if l else 48)
                    w = QKW[c]
                    cols = slice(c * P, c * P + w)
                    nc.tensor.matmul(BG[0:w, :], w_qkv[l][:, cols], hT[b][:, :], start=True, stop=False)
                    nc.tensor.matmul(BG[0:w, :], w_qkv_r[l][:, cols], hT_r[b][:, :], start=False,
                                     stop=True).then_inc(shared_full, 1)
                elif kind == "v":
                    l, b, i = args
                    for t in range(2):
                        tok = slice((2 * i + t) * P, (2 * i + t + 1) * P)
                        o = BG[:, t * C:(t + 1) * C]
                        nc.tensor.matmul(o, hT[b][:, tok], w_qkv[l][:, QK:3 * C], start=True, stop=False)
                        ins = nc.tensor.matmul(o, hT_r[b][:, tok], w_qkv_r[l][:, QK:3 * C], start=False, stop=True)
                    ins.then_inc(shared_full, 1)
                elif kind == "rowmax":
                    g, u = args
                    l, b, h = lb(g)
                    j, qt = divmod(u, NT)
                    n = MAXN[item]
                    if u == 0:
                        if g % NG == 0:
                            pe.wait_ge(stacked[g // NG][0], 16 * (NSTACK + (l > 0)))
                        elif g % NG == 1:
                            pe.wait_ge(stacked[g // NG][1], 16 * (NSTACK + (l > 0)))
                    if l == 0 and u == 0 and g % NG == 0:
                        pe.wait_ge(ones_in, 16 * (b + 1))
                    if n == 1:
                        pe.wait_ge(mod_ready, L)
                    if n > 2:
                        pe.wait_ge(rowmax_done, n - 2)
                    w = keys_of(l, qt)
                    o = SM[(n - 1) % 2]
                    q = QS[b][0:KROWS, h + j, qt * P:(qt + 1) * P]
                    ins = nc.tensor.matmul(o[:, 0:w], q, KS[b][0:KROWS, h + j, 0:w], start=True, stop=(l == 0))
                    if l:
                        ins = nc.tensor.matmul(o[:, w - P:w], identb[:, :], mask_qk[:, :], start=False, stop=True)
                    ins.then_inc(rowmax_full, 1)
                elif kind == "mT":
                    g, = args
                    pe.wait_ge(msplit_ready, g + 1)
                    for t in range(NT):
                        ins = nc.tensor.transpose(BGm[0:3 * HG, t * P:(t + 1) * P],
                                                  msp[:, t, :, :].rearrange("p s j -> p (s j)"), identb[:, :])
                    ins.then_inc(shared_full, 1)
                elif kind == "probs":
                    g, u = args
                    l, b, h = lb(g)
                    kt, pair = divmod(u, 2)
                    n = PROB[item]
                    if u == 0:
                        pe.wait_ge(m_in[g % 2], 48 * (g // 2 + 1))
                    if n == 1:
                        pe.wait_ge(gates_ready, L * B)
                    if n > 2:
                        pe.wait_ge(probs_ready, n - 2)
                    q0 = first_query(l, kt)
                    for j in range(2):
                        hh = h + 2 * pair + j
                        o = ST[(n - 1) % 2][:, j, :]
                        ins = nc.tensor.matmul(o[:, q0:T], KS[b][0:KROWS, hh, kt * P:(kt + 1) * P],
                                               QS[b][0:KROWS, hh, q0:T], start=True, stop=(l == 0))
                        if l:
                            ins = nc.tensor.matmul(o[:, q0:q0 + P], identb[:, :], mask_kq[:, :], start=False, stop=True)
                    ins.then_inc(scores_ready, 1)
                elif kind == "pv":
                    g, kt = args
                    l, b, h = lb(g)
                    n = PVN[item]
                    pe.wait_ge(probs_ready, 2 * n)
                    if kt == 0 and g:
                        pe.wait_ge(o_ready, g)
                    q0 = first_query(l, kt)
                    for j in range(HG):
                        ins = nc.tensor.matmul(OB[VW * j:VW * (j + 1), q0:T], V[b][:, kt, h + j, :],
                                               probs[:, kt % 2, j, q0:T], start=(kt == 0), stop=(kt == NT - 1))
                    ins.then_inc(pv_done, 1)
                elif kind == "o":
                    g, = args
                    pe.wait_ge(o_ready, g + 1)
                    for t in range(NT):
                        ins = nc.tensor.transpose(BG[:, t * P:(t + 1) * P], OT[:, t * P:(t + 1) * P], ident[:, :])
                    ins.then_inc(shared_full, 1)
                elif kind == "aT":
                    l, b, r = args
                    pe.wait_ge(shared_free, FREE[("o", (l * B + b + 1) * NG - 1)])
                    for t in range(NT):
                        src = at[b][:, t, P:C] if r else at[b][:, t, 0:P]
                        n = R if r else P
                        ins = nc.tensor.transpose(BG[0:n, t * P:(t + 1) * P], src, ident[:, :])
                    ins.then_inc(shared_full, 1)
                elif kind == "proj":
                    l, b, i = args
                    pe.wait_ge(gated, l * B + b + 1)
                    for t in range(2):
                        tok = slice((2 * i + t) * P, (2 * i + t + 1) * P)
                        o = BG[:, t * C:(t + 1) * C]
                        nc.tensor.matmul(o, aT[:, tok], g_proj[l][b][:, :], start=True, stop=False)
                        ins = nc.tensor.matmul(o, aT_r[:, tok], g_proj_r[l][b][:, :], start=False, stop=True)
                    ins.then_inc(shared_full, 1)
                elif kind == "fc1":
                    l, b, c = args
                    pe.wait_ge(fc1_in[l], 48)
                    w = FW[c]
                    cols = slice(c * P, c * P + w)
                    nc.tensor.matmul(BG[0:w, :], w_fc1[l][:, cols], hT[b][:, :], start=True, stop=False)
                    nc.tensor.matmul(BG[0:w, :], w_fc1_r[l][:, cols], hT_r[b][:, :], start=False,
                                     stop=True).then_inc(shared_full, 1)
                elif kind == "fc2":
                    l, b, i = args
                    pe.wait_ge(g_ready, GATE[("gate", l, b, NF - 1)])
                    for t in range(2):
                        tok = slice((2 * i + t) * P, (2 * i + t + 1) * P)
                        for c in range(NF):
                            w = FW[c] + (c == NF - 1)
                            ins = nc.tensor.matmul(BG[:, t * C:(t + 1) * C], U[0:w, c, tok], g_fc2[l][b][0:w, c, :],
                                                   start=(c == 0), stop=(c == NF - 1))
                    ins.then_inc(shared_full, 1)


def kernel(**inputs):
    import numpy as np
    from concourse import bacc
    from concourse.bass_utils import run_bass_kernel_spmd

    nc = bacc.Bacc("TRN2", target_bir_lowering=False, num_devices=1)
    arrays, aps = {}, {}
    for name, value in inputs.items():
        v = np.ascontiguousarray(np.asarray(value).T if name == "cond_1152" else value)
        arrays["in_" + name] = v
        aps[name] = nc.dram_tensor("in_" + name, v.shape, mybir.dt.from_np(v.dtype), kind="ExternalInput").ap()
    out = nc.dram_tensor("out", (B, T, C), F32, kind="ExternalOutput").ap()
    two_block_kernel(nc, aps, out)
    r = run_bass_kernel_spmd(nc, [arrays], core_ids=[0])
    return r.results[0]["out"]
```

```python
import concourse.bass as bass
import concourse.mybir as mybir
from contextlib import ExitStack

F32 = mybir.dt.float32
F32R = mybir.dt.float32r
BF16 = mybir.dt.bfloat16
U32 = mybir.dt.uint32
ALU = mybir.AluOpType
ACT = mybir.ActivationFunctionType
AX = mybir.AxisListType

P = 128
B, T, C = 2, 512, 144
L = 2
H = 16
D = C // H
FF = 4 * C
NT = T // P
R = C - P
NG = 4
HG = H // NG
QK = 2 * C
QKW = [128, 128, QK - 256]
FW = [128, 128, 128, 128, FF - 512]
NF = len(FW)
VW = D + 1
CT = 32
SR = 96
EPS = 1e-6
SCALE = float(D) ** -0.5
NEG = -1e30
GELU_C = 0.7978845608028654
GELU_A = 0.044715

Q_RUNS = [(0, 1, 3), (1, 1, 2), (2, 1, 1)]
K_RUNS = [(0, 3, 1), (0, 2, 1), (0, 1, 1)]
PRODUCTS = 6
MROW = PRODUCTS * D
KROWS = 96

SH, SC, GA = 0, 1, 2


def head_items(l, b):
    return ([("stats", l, b, 0), ("norm", l, b, 0), ("hT", l, b, 0, 1), ("hT", l, b, 0, 0)]
            + [("qk", l, b, c) for c in (2, 0, 1)] + [("v", l, b, i) for i in range(2)])


def tail_items(l, b):
    items = [("aT", l, b, 0), ("aT", l, b, 1), ("proj", l, b, 0), ("proj", l, b, 1),
             ("stats", l, b, 1), ("norm", l, b, 1), ("hT", l, b, 1, 1), ("hT", l, b, 1, 0)]
    for c in range(NF + 2):
        if c < NF:
            items.append(("fc1", l, b, c))
        if c >= 1 and c - 1 < NF:
            items.append(("tanh", l, b, c - 1))
        if c >= 2:
            items.append(("gate", l, b, c - 2))
    return items + [("fc2", l, b, 0), ("fc2", l, b, 1)]


SIDE = ([("acol", 0, 0), ("wsplit", 0, 0)] + head_items(0, 0) + head_items(0, 1)
        + tail_items(0, 0) + head_items(1, 0) + tail_items(0, 1) + head_items(1, 1)
        + tail_items(1, 0) + tail_items(1, 1))
WEIGHTS = ([("acol", 0, 1), ("wsplit", 0, 1), ("wsplit", 1, 0), ("wsplit", 1, 1), ("acol", 1, 0), ("acol", 1, 1)]
           + [("agate", l, b) for l in range(L) for b in range(B)])
GROUPS = L * B * NG
BANKS = 7


def keys_of(l, qt):
    return (qt + 1) * P if l else T


def first_query(l, kt):
    return kt * P if l else 0


def steps():
    out = []

    def add(stream, engine, item, ns, *after):
        out.append((stream, engine, item, ns, after))

    cost = {"acol": (800, 350), "agate": (1150, 370), "v": (1000, 370), "proj": (1150, 370), "fc2": (2900, 370)}
    loaded = {("acol", 0, 0): 5500, ("acol", 0, 1): 10000, ("wsplit", 0, 0): 7500, ("wsplit", 0, 1): 12000,
              ("wsplit", 1, 0): 14000, ("wsplit", 1, 1): 16000, ("acol", 1, 0): 18000, ("agate", 0, 0): 9000,
              ("agate", 1, 0): 18000}
    norm = None
    for item in SIDE + WEIGHTS:
        kind, l, *rest = item
        b = rest[0]
        stream = "side" if item in SIDE else "weights"
        if kind in cost:
            after = {"acol": [], "agate": [],
                     "v": [("DVE", ("hT", l, b, 0, 0))],
                     "proj": [("ACT", ("aT", l, b, 0)), ("ACT", ("aT", l, b, 1)), ("POOL", ("agate", l, b))],
                     "fc2": [("DVE", ("gate", l, b, NF - 1))]}[kind]
            add(stream, "PE", item, cost[kind][0], *after, loaded.get(item, 0))
            add(stream, "DVE", item, cost[kind][1], ("PE", item))
            if kind == "agate":
                add(stream, "POOL", item, 3200, ("DVE", item), 66000)
            if kind == "fc2" and l == L - 1:
                add("side", "SP", item, 500, ("DVE", item))
        elif kind == "wsplit":
            add(stream, "ACT", item, 1700, loaded[item])
            if stream == "side":
                add(stream, "DVE", item, 1100, ("ACT", item))
            else:
                add(stream, "POOL", item, 6500 if b else 3500, ("ACT", item), 25000)
        elif kind == "stats":
            k = rest[1]
            last = ("proj", l, b) if k else ("fc2", l - 1, b)
            add("side", "DVE", item, 1500, *([("DVE", (*last, i)) for i in range(2)] if l or k else []))
            add("side", "POOL", item, 960, ("DVE", item))
        elif kind == "norm":
            after = [("POOL", ("stats", *item[1:]))]
            if norm:
                after += [("PE", ("hT", *norm[1:], r)) for r in range(2)]
            norm = item
            add("side", "DVE", item, 1060, *after)
        elif kind == "hT":
            k, r = rest[1:]
            add("side", "PE", item, 250 if r else 850, ("DVE", ("norm", l, b, k)))
            add("side", "ACT", item, 660, ("PE", item), ("DVE", ("acol", l, k)))
            add("side", "DVE", item, 1350 if r else 1050, ("ACT", item))
        elif kind == "qk":
            add("side", "PE", item, 860, ("DVE", ("hT", l, b, 0, 0)), ("POOL", ("wsplit", l, 0)) if l else ("DVE", ("wsplit", 0, 0)))
            add("side", "ACT", item, 480, ("PE", item))
            add("side", "DVE", item, 1700, ("ACT", item))
            c = rest[1]
            after = [("PE", ("scores", (b + 1) * NG - 1, 15))] if l and c < 2 else []
            add("side", "SP", item, (4500, 6000, 900)[c], ("DVE", item), *after)
        elif kind == "aT":
            add("side", "PE", item, 250 if rest[1] else 450, ("DVE", ("o", (l * B + b + 1) * NG - 1)))
            add("side", "ACT", item, 480, ("PE", item))
        elif kind == "fc1":
            c = rest[1]
            mlp = [("DVE", ("gate", *((l, 0) if b else (l - 1, 1)), c))] if l or b else [("POOL", ("wsplit", 1, 1)), ("PE", ("agate", 1, B - 1))]
            add("side", "PE", item, 860, ("DVE", ("hT", l, b, 1, 0)), ("POOL", ("wsplit", l, 1)))
            add("side", "ACT", item, 960, ("PE", item), *mlp)
            if l == 0:
                add("side", "DVE", item, 1000, ("ACT", item))
        elif kind == "tanh" and l == 0:
            add("side", "ACT", item, 520, ("DVE", ("fc1", *item[1:])))
        elif kind == "gate":
            add("side", "DVE", item, 620, ("ACT", ("fc1" if l else "tanh", *item[1:])))
    for g in range(GROUPS):
        l, b = g // (B * NG), g // NG % B
        for u in range(HG * NT):
            w = keys_of(l, u % NT)
            add("max", "PE", ("max", g, u), w / 2.4 + 60 * l, ("SP", ("qk", l, b, 1)))
            add("max", "DVE", ("max", g, u), w / 0.96 + 65, ("PE", ("max", g, u)),
                *([("POOL", ("msplit", g - 2))] if g >= 2 else []))
        add("shift", "POOL", ("msplit", g), 900, ("DVE", ("max", g, 15)), *([("PE", ("mT", g - 1))] if g else []))
        add("shift", "PE", ("mT", g), 250, ("POOL", ("msplit", g)))
        add("shift", "ACT", ("mT", g), 480, ("PE", ("mT", g)))
        add("rows", "POOL", ("mT", g), 1000, ("ACT", ("mT", g)))
        for u in range(HG * NT):
            kt = u // HG
            w = T - first_query(l, kt)
            n = g * NT + kt
            add("attend", "PE", ("scores", g, u), w / 2.4 + 60 * l, ("rows", ("mT", g)))
            add("attend", "ACT", ("scores", g, u), w / 1.2 + 60, ("PE", ("scores", g, u)),
                *([("PE", ("pv", (n - 2) // NT, (n - 2) % NT))] if n >= 2 else []))
            if u % HG == HG - 1:
                add("gather", "PE", ("pv", g, kt), w * 1.7 + 140, ("ACT", ("scores", g, u)),
                    *([("ACT", ("oT", g - 1))] if g and kt == 0 else []))
        add("gather", "ACT", ("oT", g), 480, ("PE", ("pv", g, NT - 1)), *([("PE", ("o", g - 1))] if g else []))
        add("gather", "PE", ("o", g), 450, ("ACT", ("oT", g)))
        add("gather", "DVE", ("o", g), 500, ("PE", ("o", g)))
    return out


READER = {"hT": "ACT", "qk": "DVE", "fc1": "ACT", "aT": "ACT", "mT": "ACT", "scores": "ACT"}
ENGINES = ("PE", "ACT", "DVE", "POOL", "SP")
HOLD = {"attend": 3, "max": 3}
OTHERS, CALM = 2, 5
HANDOVER = 150
WINDOW = 0


def plan():
    queues, cost, after, behind, inf = {}, {}, {}, {}, float("inf")
    for stream, engine, item, ns, follows in steps():
        queue = queues.setdefault((engine, stream), [])
        cost[engine, item], after[engine, item] = ns, follows
        for follow in [*follows, *((engine, last) for last in queue[-1:])]:
            if not isinstance(follow, int):
                behind.setdefault(("POOL", follow[1]) if follow[0] == "rows" else follow, []).append((engine, item))
        queue.append(item)
    urgency = {}

    def chain_from(step):
        stack = [step]
        while stack:
            top = stack[-1]
            open_ones = [x for x in behind.get(top, []) if x not in urgency]
            if open_ones:
                stack.extend(open_ones)
            else:
                urgency[top] = cost[top] + HANDOVER * 0 + max([urgency[x] for x in behind.get(top, [])], default=0)
                stack.pop()

    for step in cost:
        if step not in urgency:
            chain_from(step)
    at = {q: 0 for q in queues}
    free = {engine: 0 for engine in ENGINES}
    done, order = {}, {engine: [] for engine in ENGINES}
    bank, before, holder = {}, {}, [(None, None)] * BANKS
    while any(at[q] < len(items) for q, items in queues.items()):
        best = None
        for engine in ENGINES:
            mine_best = []
            for q in queues:
                stream = q[1]
                if q[0] != engine or at[q] == len(queues[q]):
                    continue
                item = queues[q][at[q]]
                ends = []
                for follow in after[engine, item]:
                    if isinstance(follow, int):
                        ends.append(follow)
                    elif follow[0] == "rows":
                        ends.append(done.get(("POOL", follow[1]), inf) + 2000 + HANDOVER)
                    else:
                        ends.append(done.get(follow, inf) + HANDOVER)
                start = max([free[engine], *ends])
                if start == inf:
                    continue
                k = None
                if engine == "PE" and item[0] != "pv":
                    left = [None if i is None else done.get((READER.get(i[0], "DVE"), i)) for i, _ in holder]
                    holds = [s == stream and i is not None and (t is None or t > start)
                             for (i, s), t in zip(holder, left)]
                    group = stream if stream in HOLD else "other"
                    others = [s not in HOLD and i is not None and (t is None or t > start)
                              for (i, s), t in zip(holder, left)]
                    calm = at["PE", "max"] == 0 or at["PE", "attend"] == len(queues["PE", "attend"])
                    used = sum(others) if group == "other" else sum(holds)
                    if used >= HOLD.get(group, CALM if calm else OTHERS):
                        mine = [t for h, t in zip(others if group == "other" else holds, left) if h and t is not None]
                        if not mine:
                            continue
                        start = max(start, min(mine) + HANDOVER)
                    ready = [(0 if i is None else t, n) for n, ((i, _), t) in enumerate(zip(holder, left))
                             if i is None or t is not None]
                    if not ready:
                        continue
                    t, k = min(ready)
                    start = max(start, t + HANDOVER if holder[k][0] else 0)
                mine_best.append((start, -urgency[engine, item], engine, stream, item, k))
            if mine_best:
                first = min(mine_best)[0]
                chosen = min((c for c in mine_best if c[0] <= first + WINDOW), key=lambda c: c[1])
                if best is None or chosen[0] < best[0]:
                    best = chosen
        start, _, engine, stream, item, k = best
        at[engine, stream] += 1
        free[engine] = done[engine, item] = start + cost[engine, item]
        order[engine].append(item)
        if k is not None:
            bank[item] = k
            if holder[k][0]:
                before[item] = holder[k][0]
            holder[k] = (item, stream)
    return order, bank, before


ORDER, BANK, BEFORE = plan()


def ordinals(kinds):
    return {item: n for n, item in enumerate((item for item in SIDE if item[0] in kinds), 1)}


def two_block_kernel(nc, a, out):
    ctx = ExitStack()

    def sb(name, shape, dt=F32):
        return ctx.enter_context(nc.sbuf_tensor(name, shape, dt))

    def ps(name, shape):
        return ctx.enter_context(nc.psum_tensor(name, shape, F32))

    def sem(name):
        return ctx.enter_context(nc.semaphore(name))

    with ctx:
        ident = sb("ident", [P, P])
        identb = sb("identb", [P, P], BF16)
        mask_qk = sb("mask_qk", [P, P], BF16)
        mask_kq = sb("mask_kq", [P, P], BF16)
        onesb = sb("onesb", [P, T], BF16)
        zerosb = sb("zerosb", [P, T], BF16)
        w_qk = [[sb(f"w_qk{l}{i}", [P, QK], F32R) for i in range(2)] for l in range(L)]
        w_v = [sb(f"w_v{l}", [P, C]) for l in range(L)]
        w_qkv_s = [sb(f"w_qkv_s{l}", [SR, 3 * C], F32R) for l in range(L)]
        w_fc1 = [[sb(f"w_fc1{l}{i}", [P, FF], F32R) for i in range(2)] for l in range(L)]
        w_fc1_s = [sb(f"w_fc1_s{l}", [SR, FF], F32R) for l in range(L)]
        w_proj = [sb(f"w_proj{l}", [P, C]) for l in range(L)]
        w_proj_r = [sb(f"w_proj_r{l}", [R + 1, C]) for l in range(L)]
        w_fc2 = [sb(f"w_fc2{l}", [P, NF, C]) for l in range(L)]
        g_proj = [[sb(f"g_proj{l}{b}", [P, C]) for b in range(B)] for l in range(L)]
        g_proj_r = [[sb(f"g_proj_r{l}{b}", [SR, C]) for b in range(B)] for l in range(L)]
        g_fc2 = [[sb(f"g_fc2{l}{b}", [P, NF, C]) for b in range(B)] for l in range(L)]
        cond = sb("cond", [P, 4, B])
        cond_r = sb("cond_r", [R + 1, 4, B])
        cond_w = sb("cond_w", [P, B, P])
        cond_wr = sb("cond_wr", [R + 1, B, P])
        mod = [sb(f"mod{l}", [P, 2, 2, B]) for l in range(L)]
        mod_r = [sb(f"mod_r{l}", [R, 2, 2, B]) for l in range(L)]
        X = [sb(f"X{b}", [P, NT, C]) for b in range(B)]
        stat = sb("stat", [P, NT, 6])
        mean = sb("mean", [P, NT, 2])
        veps = sb("veps", [P, NT])
        rstd = sb("rstd", [P, NT])
        half = sb("half", [P, NT])
        hn = sb("hn", [P, NT, C])
        hT = sb("hT", [P, T])
        hT_p = [sb(f"hT_p{i}", [P, T], F32R) for i in range(2)]
        hT_r = sb("hT_r", [R, T])
        hT_s = sb("hT_s", [SR, T], F32R)
        parts = sb("parts", [P, 3, 3, T], BF16)
        rest = sb("rest", [P, T])
        QS = [sb(f"QS{b}", [P, H, T], BF16) for b in range(B)]
        KS = [sb(f"KS{b}", [P, H, T], BF16) for b in range(B)]
        gates = [[sb(f"gates{l}{b}", [P, 2, C]) for b in range(B)] for l in range(L)]
        V = [sb(f"V{b}", [P, NT, H, VW]) for b in range(B)]
        probs = sb("probs", [P, 2, HG, T])
        negm = sb("negm", [P, 2, NT, HG])
        mrest = sb("mrest", [P, NT, HG])
        msp = sb("msp", [P, NT, 3, HG], BF16)
        mT = sb("mT", [3 * HG, 2, T], BF16)
        OT = sb("OT", [P, T])
        rden = sb("rden", [P, NT, HG])
        at = [sb(f"at{b}", [P, NT, C]) for b in range(B)]
        aT = sb("aT", [P, T])
        aT_r = sb("aT_r", [SR, T])
        xh = sb("xh", [P, NF, T])
        U = sb("U", [P, NF, T])
        ada_cols = L * 6 * C
        flat_xh, flat_U = (t[:, :, :].rearrange("p c t -> p (c t)") for t in (xh, U))
        w_ada = [flat_xh[:, l * 6 * C:(l + 1) * 6 * C] for l in range(L)]
        w_ada_r = [flat_U[0:R + 1, l * 6 * C:(l + 1) * 6 * C] for l in range(L)]
        flat_at = [t[:, :, :].rearrange("p t c -> p (t c)") for t in at]
        raw = [[flat_at[0][:, 0:QK], flat_at[1][:, :]],
               [flat_at[0][:, QK:2 * QK], flat_xh[:, ada_cols:ada_cols + FF]]]
        raw_r = [[(aT[0:R + 1, 0:3 * C], OT[0:R + 1, 0:3 * C])[l],
                  g_fc2[1][l][0:R + 1, :, :].rearrange("p c n -> p (c n)")[:, 0:FF]] for l in range(L)]

        PB = [ps(f"PB{k}", [P, T]) for k in range(BANKS)]
        OB = ps("OB", [P, T])

        def bank_of(item):
            return PB[BANK[item]][:, :]

        scratch = nc.dram_tensor("qk_parts", [L, B, 2, 3, D, H, T], BF16, kind="Internal").ap()

        cond_in = sem("cond_in")
        ada_in = [[sem(f"ada_in{l}{k}") for k in range(2 - l)] for l in range(L)]
        x_in = [sem(f"x_in{b}") for b in range(B)]
        qkv_in = [sem(f"qkv_in{l}") for l in range(L)]
        proj_in = [sem(f"proj_in{l}") for l in range(L)]
        fc1_in = [sem(f"fc1_in{l}") for l in range(L)]
        rows_zero = sem("rows_zero")
        filled_first = sem("filled_first")
        filled = sem("filled")
        q_zeroed = [sem(f"q_zeroed{b}") for b in range(B)]
        k_zeroed = [sem(f"k_zeroed{b}") for b in range(B)]
        filled_late = sem("filled_late")
        consts = sem("consts")
        pool_step = sem("pool_step")
        dve_step = sem("dve_step")
        th_ready = sem("th_ready")
        silu_ready = sem("silu_ready")
        high_w = sem("high_w")
        low_w = [sem(f"low_w{l}{k}") for l in range(L) for k in range(2)]
        wide_ready = sem("wide_ready")
        split = sem("split")
        gw_filled = sem("gw_filled")
        gated = sem("gated")
        outputs_filled = sem("outputs_filled")
        stats_ready = sem("stats_ready")
        rstd_ready = sem("rstd_ready")
        normed = sem("normed")
        bank_full = [sem(f"bank_full{k}") for k in range(BANKS)]
        bank_free = [sem(f"bank_free{k}") for k in range(BANKS)]
        high_ready = sem("high_ready")
        parts_ready = sem("parts_ready")
        parts_out = sem("parts_out")
        stacked = [[sem(f"stacked{p}{i}") for i in range(2)] for p in range(L * B)]
        msplit_ready = sem("msplit_ready")
        m_in = [sem(f"m_in{i}") for i in range(2)]
        pv_done = sem("pv_done")
        o_ready = sem("o_ready")
        u_ready = sem("u_ready")
        t_ready = sem("t_ready")
        g_ready = sem("g_ready")
        stored = sem("stored")

        nth = {}
        for k in range(BANKS):
            for n, i in enumerate((i for i in ORDER["PE"] if BANK.get(i) == k), 1):
                nth[i] = n
        STATS = ordinals(("stats",))
        NORM = ordinals(("norm",))
        QKN = ordinals(("qk",))
        GATE = ordinals(("gate",))
        HTN = ordinals(("hT",))
        GELU_U = {i: n for n, i in enumerate((i for i in SIDE if i[0] == "fc1" and i[1] == 0), 1)}
        NSTACK = len(Q_RUNS) + len(K_RUNS)

        def full(eng, item):
            eng.wait_ge(bank_full[BANK[item]], nth[item])

        def released(eng, item):
            eng.wait_ge(bank_free[BANK[item]], nth[item])

        def attended(eng, g, kt):
            eng.wait_ge(pv_done, g * NT + kt + 1)

        def before(l, b):
            return (l, 0) if b else (l - 1, 1)

        def lb(g):
            return g // (B * NG), g // NG % B, g % NG * HG

        def by_part(w):
            v = w.rearrange("p (s h d) -> p s d h", s=2, h=H)
            return v[:, :, 0:D - 1, :], v[:, :, D - 1, :]

        def in_part(w):
            return (w[:, 0:2 * P].rearrange("p (s d h) -> p s d h", s=2, h=H),
                    w[:, 2 * P:QK].rearrange("p (s h) -> p s h", s=2))

        def pieces(l, k):
            n = R + 1
            if k:
                s, r = w_fc1_s[l], raw_r[l][1]
                return [(raw[l][1], w_fc1[l][0][:, :], w_fc1[l][1][:, :]), (r, s[0:n, :], s[64:64 + n, :])]
            s, r = w_qkv_s[l], raw_r[l][0]
            out = [*zip(by_part(raw[l][0]), in_part(w_qk[l][0][:, :]), in_part(w_qk[l][1][:, :]))]
            out += [*zip(by_part(r[:, 0:QK]), in_part(s[0:n, 0:QK]), in_part(s[64:64 + n, 0:QK]))]
            return out + [(r[:, QK:], s[0:n, QK:], s[64:64 + n, QK:])]

        def low_values(eng, l, k, link):
            for n, (whole, high, low) in enumerate(pieces(l, k), 1):
                ins = eng.tensor_tensor(low, whole, high.bitcast(F32), ALU.subtract)
                if n < len(pieces(l, k)):
                    link(ins)
            return ins

        block = ctx.enter_context(nc.Block())

        @block.sync
        def _(sp):
            sp.dma_start(cond[:, 0, :], a["cond_1152"][0:P]).then_inc(cond_in, 16)
            sp.dma_start(cond_r[0:R, 0, :], a["cond_1152"][P:C]).then_inc(cond_in, 16)
            row = lambda v: v.rearrange("(a n) -> a n", a=1)
            ada = [("L0_cond_W_ada", "L0_cond_b_ada"), ("L1_cond_Wa", "L1_cond_ba")]
            qkv = [[("L0_cond_W_qkv", i * C) for i in range(3)], [("L1_cond_Wq", 0), ("L1_cond_Wk", 0), ("L1_cond_Wv", 0)]]

            def load_ada(l, k, n=1):
                w, bias = (a[name] for name in ada[l])
                cols = slice(k * 3 * C, (k + n) * 3 * C)
                sp.dma_start(w_ada[l][:, cols], w[0:P, cols]).then_inc(ada_in[l][k], 16)
                sp.dma_start(w_ada_r[l][0:R, cols], w[P:C, cols]).then_inc(ada_in[l][k], 16)
                sp.dma_start(w_ada_r[l][R:R + 1, cols], row(bias)[:, cols]).then_inc(ada_in[l][k], 16)

            def load_x(b):
                sp.dma_start(X[b][:, :, :], a["x"][b].rearrange("(t p) c -> p t c", p=P)).then_inc(x_in[b], 16)

            load_x(0)
            load_ada(0, 0)
            w = a["L0_cond_W_qkv"]
            sp.dma_start(raw[0][0], w[0:P, 0:QK]).then_inc(qkv_in[0], 16)
            sp.dma_start(raw_r[0][0][0:R], w[P:C, :]).then_inc(qkv_in[0], 16)
            sp.dma_start(raw_r[0][0][R:R + 1], row(a["L0_cond_b_qkv"])).then_inc(qkv_in[0], 16)
            sp.dma_start(w_v[0][:, :], w[0:P, QK:3 * C]).then_inc(qkv_in[0], 16)
            load_ada(0, 1)
            load_x(1)
            sp.wait_ge(filled, 1)
            names = [("L0_cond_W_proj", "L0_cond_b_proj", "L0_cond_W_fc1", "L0_cond_b_fc1",
                      "L0_cond_W_fc2", "L0_cond_b_fc2"),
                     ("L1_cond_Wp", "L1_cond_bp", "L1_cond_W1", "L1_cond_b1", "L1_cond_W2", "L1_cond_b2")]

            def load_fc1(l):
                w1, b1 = (a[n] for n in names[l][2:4])
                sp.dma_start(raw[l][1], w1[0:P, :]).then_inc(fc1_in[l], 16)
                sp.dma_start(raw_r[l][1][0:R], w1[P:C, :]).then_inc(fc1_in[l], 16)
                sp.dma_start(raw_r[l][1][R:R + 1], row(b1)).then_inc(fc1_in[l], 16)

            def load_out(l):
                wp, bp, _, _, w2, b2 = (a[n] for n in names[l])
                sp.dma_start(w_proj[l][:, :], wp[0:P, :]).then_inc(proj_in[l], 16)
                sp.dma_start(w_proj_r[l][0:R], wp[P:C, :]).then_inc(proj_in[l], 16)
                sp.dma_start(w_proj_r[l][R:R + 1], row(bp)).then_inc(proj_in[l], 16)
                sp.dma_start(w_fc2[l][:, 0:4, :], w2[0:4 * P, :].rearrange("(c p) n -> p c n", p=P)).then_inc(proj_in[l], 16)
                sp.dma_start(w_fc2[l][0:FW[4], 4, :], w2[4 * P:FF, :]).then_inc(proj_in[l], 16)
                sp.dma_start(w_fc2[l][FW[4]:FW[4] + 1, 4, :], row(b2)).then_inc(proj_in[l], 16)

            def load_rest(part):
                if part == 0:
                    load_fc1(0)
                    for i, name in enumerate(("L1_cond_Wq", "L1_cond_Wk")):
                        sp.dma_start(raw[1][0][:, i * C:(i + 1) * C], a[name][0:P, :]).then_inc(qkv_in[1], 16)
                    for i, name in enumerate(("L1_cond_Wq", "L1_cond_Wk", "L1_cond_Wv")):
                        sp.dma_start(raw_r[1][0][0:R, i * C:(i + 1) * C], a[name][P:C, :]).then_inc(qkv_in[1], 16)
                    sp.dma_start(w_v[1][:, :], a["L1_cond_Wv"][0:P, :]).then_inc(qkv_in[1], 16)
                    load_fc1(1)
                    load_ada(1, 0, 2)
                else:
                    load_out(0)
                    load_out(1)

            load_rest(0)

            for item in ORDER["SP"]:
                kind, *args = item
                if kind == "qk":
                    l, b, c = args
                    sp.wait_ge(parts_ready, QKN[item])
                    if c == 2:
                        for i in range(2):
                            sp.dma_start(scratch[l, b, i, :, D - 1].rearrange("s h t -> h s t"),
                                         parts[i * H:(i + 1) * H, 2, :, :]).then_inc(parts_out, 16)
                        continue
                    sp.dma_start(scratch[l, b, c, :, 0:D - 1].rearrange("s d h t -> (d h) s t"),
                                 parts[:, c, :, :]).then_inc(parts_out, 16)
                    sp.wait_ge(parts_out, 64 * (l * B + b) + 48 + 16 * c)
                    if c == 0:
                        sp.wait_ge(rows_zero, 2)
                    if l:
                        full(sp, ("scores", (b + 1) * NG - 1, HG * NT - 1))
                    else:
                        sp.wait_ge((k_zeroed if c else q_zeroed)[b], 1)
                    dst, runs = (KS[b], K_RUNS) if c else (QS[b], Q_RUNS)
                    if l == 0 and c:
                        sp.dma_start(dst[MROW:MROW + 3, :, :],
                                     onesb[0:3, None, :].to_broadcast([3, H, T])).then_inc(stacked[b][0], 16)
                    for i, (h0, h1) in enumerate(((0, HG), (HG, H))):
                        done = stacked[l * B + b][i]
                        row0 = 0
                        for first, n, times in runs:
                            src = scratch[l, b, c, first:first + n, :, h0:h1, :]
                            if times > 1:
                                src = src.to_broadcast([times, D, h1 - h0, T])
                            rows = D * n * times
                            sp.dma_start(dst[row0:row0 + rows, h0:h1, :], src).then_inc(done, 16)
                            row0 += rows
                        if l and c == 0:
                            sp.dma_start(dst[MROW:MROW + 3, h0:h1, :],
                                         zerosb[0:3, None, :].to_broadcast([3, h1 - h0, T])).then_inc(done, 16)
                    if (l, b, c) == (0, 0, 1):
                        load_rest(1)
                elif kind == "fc2":
                    l, b, i = args
                    released(sp, item)
                    sp.dma_start(out[b, 2 * i * P:2 * (i + 1) * P, :].rearrange("(t p) c -> p t c", p=P),
                                 X[b][:, 2 * i:2 * i + 2, :]).then_inc(stored, 16)
            sp.wait_ge(stored, 16 * 2 * B)

        @block.gpsimd
        def _(pool):
            chain = [0]

            def link(ins):
                chain[0] += 1
                ins.then_inc(pool_step, 1)
                pool.wait_ge(pool_step, chain[0])

            nc.gpsimd.memset(ident[:, :], 0.0)
            nc.gpsimd.memset(identb[:, :], 0.0)
            nc.gpsimd.memset(mask_qk[:, :], 0.0)
            link(nc.gpsimd.memset(mask_kq[:, :], 0.0))
            nc.gpsimd.affine_select(out=ident[:, :], in_=ident[:, :], compare_op=ALU.not_equal, fill=1.0,
                                    base=0, pattern=[[-1, P]], channel_multiplier=1)
            nc.gpsimd.affine_select(out=identb[:, :], in_=identb[:, :], compare_op=ALU.not_equal, fill=1.0,
                                    base=0, pattern=[[-1, P]], channel_multiplier=1)
            nc.gpsimd.memset(half[:, :], -0.5).then_inc(consts, 1)
            nc.gpsimd.affine_select(out=mask_qk[:, :], in_=mask_qk[:, :], compare_op=ALU.is_ge, fill=NEG,
                                    base=0, pattern=[[-1, P]], channel_multiplier=1)
            nc.gpsimd.affine_select(out=mask_kq[:, :], in_=mask_kq[:, :], compare_op=ALU.is_ge, fill=NEG,
                                    base=0, pattern=[[1, P]], channel_multiplier=-1).then_inc(consts, 1)

            nc.gpsimd.memset(raw_r[1][0], 0.0)
            nc.gpsimd.memset(w_qkv_s[1][:, :].bitcast(F32), 0.0)
            for l in range(L):
                ins = nc.gpsimd.memset(w_fc1_s[l][:, :].bitcast(F32), 0.0)
            ins.then_inc(filled, 1)
            nc.gpsimd.memset(onesb[0:3, :], 1.0).then_inc(rows_zero, 1)
            nc.gpsimd.memset(zerosb[0:3, :], 0.0).then_inc(rows_zero, 1)

            def gate_weights(l, b):
                released(pool, ("agate", l, b))
                pool.wait_ge(proj_in[l], 16 * 6)
                pool.wait_ge(gw_filled, 1)
                g = gates[l][b]
                nc.gpsimd.tensor_tensor(g_proj[l][b][:, :], w_proj[l][:, :], g[:, 0, :], ALU.mult)
                nc.gpsimd.tensor_tensor(g_proj_r[l][b][0:R + 1, :], w_proj_r[l][:, :], g[0:R + 1, 0, :], ALU.mult)
                for c in range(NF):
                    w = FW[c] + (c == NF - 1)
                    last = nc.gpsimd.tensor_tensor(g_fc2[l][b][0:w, c, :], w_fc2[l][0:w, c, :], g[0:w, 1, :], ALU.mult)
                last.then_inc(gated, 1)

            for item in ORDER["POOL"]:
                kind, *args = item
                if kind == "stats":
                    l, b, k = args
                    pool.wait_ge(stats_ready, STATS[item])
                    if STATS[item] == 1:
                        pool.wait_ge(consts, 1)
                    nc.gpsimd.tensor_tensor(rstd[:, :], veps[:, :], half[:, :], ALU.pow).then_inc(rstd_ready, 1)
                    if STATS[item] == 1:
                        for i in range(B):
                            nc.gpsimd.memset(QS[i][0:KROWS, :, :].bitcast(U32), 0).then_inc(q_zeroed[i], 1)
                            nc.gpsimd.memset(KS[i][0:KROWS, :, :].bitcast(U32), 0).then_inc(k_zeroed[i], 1)
                        for i in range(L):
                            for j in range(B):
                                ins = nc.gpsimd.memset(g_proj_r[i][j][:, :], 0.0)
                        link(ins)
                        for i in range(L):
                            for j in range(B):
                                ins = nc.gpsimd.memset(g_fc2[i][j][64:SR, NF - 1, :], 0.0)
                        ins.then_inc(gw_filled, 1)
                        nc.gpsimd.memset(U[64:SR, NF - 1, :], 1.0).then_inc(filled_late, 1)
                        pool.wait_ge(filled_late, 1)
                elif kind == "wsplit":
                    l, k = args
                    pool.wait_ge(high_w, 2 * l + k + 1)
                    low_values(nc.gpsimd, l, k, link).then_inc(low_w[2 * l + k], 1)
                    pool.wait_ge(low_w[2 * l + k], 1)
                elif kind == "agate":
                    gate_weights(*args)
                elif kind == "msplit":
                    g, = args
                    released(pool, ("max", g, HG * NT - 1))
                    if g:
                        full(pool, ("mT", g - 1))
                    m = negm[:, g % 2, :, :]
                    link(nc.gpsimd.tensor_copy(msp[:, :, 0, :], m))
                    link(nc.gpsimd.tensor_tensor(mrest[:, :, :], m, msp[:, :, 0, :], ALU.subtract))
                    link(nc.gpsimd.tensor_copy(msp[:, :, 1, :], mrest[:, :, :]))
                    nc.gpsimd.tensor_tensor(msp[:, :, 2, :], mrest[:, :, :], msp[:, :, 1, :],
                                            ALU.subtract).then_inc(msplit_ready, 1)
                elif kind == "mT":
                    g, = args
                    l, b, h = lb(g)
                    released(pool, item)
                    pool.dma_start(QS[b][MROW:MROW + 3, h:h + HG, :], mT[:, g % 2, :]).then_inc(m_in[g % 2], 16)

        @block.scalar
        def _(act):
            act.wait_ge(silu_ready, 1)
            nc.scalar.activation(cond[:, 2, :], cond[:, 1, :], ACT.Tanh)
            nc.scalar.activation(cond_r[0:R, 2, :], cond_r[0:R, 1, :], ACT.Tanh).then_inc(th_ready, 1)
            for item in ORDER["ACT"]:
                kind, *args = item
                if kind == "wsplit":
                    l, k = args
                    act.wait_ge(fc1_in[l] if k else qkv_in[l], 48 if k else (96 if l else 64))
                    act.wait_ge(filled if l or k else filled_first, 1)
                    for whole, high, low in pieces(l, k):
                        nc.scalar.activation(high, whole, ACT.Copy)
                    r, s = raw_r[l][k], (w_qkv_s, w_fc1_s)[k][l]
                    if k:
                        ins = nc.scalar.activation(s[32:32 + R + 1, :], r, ACT.Copy)
                    else:
                        for v, w in zip(by_part(r[:, 0:QK]), in_part(s[32:32 + R + 1, 0:QK])):
                            nc.scalar.activation(w, v, ACT.Copy)
                        ins = nc.scalar.activation(s[32:32 + R + 1, QK:], r[:, QK:], ACT.Copy)
                    ins.then_inc(high_w, 1)
                elif kind == "hT":
                    l, b, k, r = args
                    full(act, item)
                    released(act, ("acol", l, k))
                    m = (mod_r if r else mod)[l]
                    dst, n = (hT_r, R) if r else (hT, P)
                    nc.scalar.activation(dst[:, :], bank_of(item)[0:n, :], ACT.Identity, scale=m[:, k, SC, b:b + 1],
                                         bias=m[:, k, SH, b:b + 1]).then_inc(bank_free[BANK[item]], 1)
                elif kind == "qk":
                    l, b, c = args
                    full(act, item)
                    if QKN[item] > 3:
                        act.wait_ge(parts_out, 64 * ((QKN[item] - 1) // 3))
                    w = QKW[c]
                    nc.scalar.activation(parts[0:w, c, 0, :], bank_of(item)[0:w, :], ACT.Copy).then_inc(high_ready, 1)
                elif kind == "mT":
                    g, = args
                    full(act, item)
                    if g >= 2:
                        act.wait_ge(m_in[g % 2], 16 * (g // 2))
                    nc.scalar.activation(mT[:, g % 2, :], bank_of(item).bitcast(BF16)[0:3 * HG, 0:T],
                                         ACT.Copy).then_inc(bank_free[BANK[item]], 1)
                elif kind == "scores":
                    g, u = args
                    kt, j = divmod(u, HG)
                    full(act, item)
                    if g * NT + kt >= 2:
                        attended(act, *divmod(g * NT + kt - 2, NT))
                    q0 = first_query(g // (B * NG), kt)
                    nc.scalar.activation(probs[:, kt % 2, j, q0:T], bank_of(item)[:, q0:T],
                                         ACT.Exp, scale=SCALE).then_inc(bank_free[BANK[item]], 1)
                elif kind == "oT":
                    g, = args
                    attended(act, g, NT - 1)
                    if g:
                        full(act, ("o", g - 1))
                    if g == 0:
                        act.wait_ge(low_w[2], 1)
                    nc.scalar.activation(OT[:, :], OB[:, :], ACT.Copy).then_inc(o_ready, 1)
                elif kind == "aT":
                    l, b, r = args
                    full(act, item)
                    if (l, b, r) == (0, 0, 1):
                        act.wait_ge(outputs_filled, 1)
                    dst, n = (aT_r[0:R, :], R) if r else (aT[:, :], P)
                    nc.scalar.activation(dst, bank_of(item)[0:n, :], ACT.Copy).then_inc(bank_free[BANK[item]], 1)
                elif kind == "fc1":
                    l, b, c = args
                    full(act, item)
                    last_use = ("gate", *before(l, b), c)
                    if last_use in GATE:
                        act.wait_ge(g_ready, GATE[last_use])
                    if (l, b, c) == (0, 0, 0):
                        act.wait_ge(low_w[3], 1)
                        full(act, ("acol", 1, 1))
                        full(act, ("agate", 1, B - 1))
                    w = FW[c]
                    nc.scalar.activation(U[0:w, c, :], bank_of(item)[0:w, :], ACT.Tanh if l else ACT.Square, scale=0.5)
                    nc.scalar.activation(xh[0:w, c, :], bank_of(item)[0:w, :], ACT.Copy,
                                         scale=0.5).then_inc(bank_free[BANK[item]], 1)
                elif kind == "tanh":
                    l, b, c = args
                    act.wait_ge(u_ready, GELU_U[("fc1", l, b, c)])
                    w = FW[c]
                    nc.scalar.activation(U[0:w, c, :], U[0:w, c, :], ACT.Tanh).then_inc(t_ready, 1)

        @block.vector
        def _(dve):
            chain = [0]

            def link(ins):
                chain[0] += 1
                ins.then_inc(dve_step, 1)
                dve.wait_ge(dve_step, chain[0])

            nc.vector.memset(cond_r[:, 3, :], 1.0)
            nc.vector.memset(w_qkv_s[0][:, :].bitcast(F32), 0.0).then_inc(filled_first, 1)
            dve.wait_ge(cond_in, 32)
            nc.vector.tensor_scalar(cond[:, 1, :], cond[:, 0, :], 0.5, None, ALU.mult)
            nc.vector.tensor_scalar(cond_r[0:R, 1, :], cond_r[0:R, 0, :], 0.5, None, ALU.mult).then_inc(silu_ready, 1)
            nc.vector.memset(hT_s[0:32, :].bitcast(F32), 1.0)
            nc.vector.memset(hT_s[32:64, :].bitcast(F32), 0.0)
            nc.vector.memset(hT_s[64:SR, :].bitcast(F32), 1.0)
            dve.wait_ge(th_ready, 1)
            dve.wait_ge(silu_ready, 1)
            nc.vector.scalar_tensor_tensor(cond[:, 3, :], cond[:, 2, :], 1.0, cond[:, 1, :], ALU.add, ALU.mult)
            nc.vector.scalar_tensor_tensor(cond_r[0:R, 3, :], cond_r[0:R, 2, :], 1.0, cond_r[0:R, 1, :],
                                           ALU.add, ALU.mult).then_inc(silu_ready, 1)
            dve.wait_ge(silu_ready, 2)
            for b in range(B):
                nc.vector.tensor_copy(cond_w[:, b, :], cond[:, 3, b:b + 1].to_broadcast([P, P]))
                ins = nc.vector.tensor_copy(cond_wr[:, b, :], cond_r[:, 3, b:b + 1].to_broadcast([R + 1, P]))
            ins.then_inc(wide_ready, 1)

            for b in range(B):
                nc.vector.memset(V[b][:, :, :, D:VW], 1.0)
            nc.vector.memset(OB[:, :], 0.0)
            nc.vector.memset(aT_r[:, :], 1.0).then_inc(outputs_filled, 1)

            last_norm = None
            for item in ORDER["DVE"]:
                kind, *args = item
                bank = bank_of(item) if item in BANK else None
                if kind == "wsplit":
                    dve.wait_ge(high_w, 1)
                    low_values(nc.vector, 0, 0, lambda ins: None).then_inc(low_w[0], 1)
                elif kind == "acol":
                    l, k = args
                    full(dve, item)
                    for dst, n, at0 in ((mod[l], P, 0), (mod_r[l], R, 2 * B)):
                        nc.vector.tensor_copy(dst[:, k, SH, :], bank[0:n, at0:at0 + B])
                        ins = nc.vector.tensor_scalar(dst[:, k, SC, :], bank[0:n, at0 + B:at0 + 2 * B], 1.0, None, ALU.add)
                    ins.then_inc(bank_free[BANK[item]], 1)
                elif kind == "agate":
                    l, b = args
                    full(dve, item)
                    nc.vector.tensor_copy(gates[l][b][:, :, :], bank[:, 0:2 * C].rearrange("p (k c) -> p k c", k=2)
                                          ).then_inc(bank_free[BANK[item]], 1)
                elif kind == "stats":
                    l, b, k = args
                    if (l, k) == (0, 0):
                        dve.wait_ge(x_in[b], 16)
                    else:
                        for i in range(2):
                            released(dve, ("proj", l, b, i) if k else ("fc2", l - 1, b, i))
                    for t in range(NT):
                        ins = nc.vector.bn_stats(stat[:, t, :], X[b][:, t, :])
                    link(ins)
                    for t in range(NT):
                        ins = nc.vector.bn_aggr(mean[:, t, :], stat[:, t, :])
                    link(ins)
                    nc.vector.tensor_scalar(veps[:, :], mean[:, :, 1], EPS, None, ALU.add).then_inc(stats_ready, 1)
                elif kind == "norm":
                    l, b, k = args
                    dve.wait_ge(rstd_ready, STATS[("stats", l, b, k)])
                    dve.wait_ge(stats_ready, STATS[("stats", l, b, k)])
                    if last_norm:
                        for r in range(2):
                            full(dve, ("hT", *last_norm[1:], r))
                    last_norm = item
                    for t in range(NT):
                        ins = nc.vector.tensor_scalar(hn[:, t, :], X[b][:, t, :], mean[:, t, 0:1],
                                                      rstd[:, t:t + 1], ALU.subtract, ALU.mult)
                    ins.then_inc(normed, 1)
                elif kind == "hT":
                    l, b, k, r = args
                    released(dve, item)
                    if r:
                        nc.vector.tensor_copy(hT_s[64:64 + R, :], hT_r[:, :])
                        link(nc.vector.tensor_copy(hT_s[0:R, :], hT_r[:, :]))
                        nc.vector.tensor_tensor(hT_s[32:32 + R, :], hT_r[:, :], hT_s[0:R, :].bitcast(F32),
                                                ALU.subtract).then_inc(split, 1)
                    else:
                        link(nc.vector.tensor_copy(hT_p[0][:, :], hT[:, :]))
                        nc.vector.tensor_tensor(hT_p[1][:, :], hT[:, :], hT_p[0][:, :].bitcast(F32),
                                                ALU.subtract).then_inc(split, 1)
                elif kind == "qk":
                    l, b, c = args
                    w = QKW[c]
                    dve.wait_ge(high_ready, QKN[item])
                    if QKN[item] > 1:
                        dve.wait_ge(parts_ready, QKN[item] - 1)
                    hi, mid, lo = (parts[0:w, c, i, :] for i in range(3))
                    nc.vector.tensor_tensor(rest[0:w, :], bank[0:w, :], hi, ALU.subtract).then_inc(bank_free[BANK[item]], 1)
                    released(dve, item)
                    link(nc.vector.tensor_copy(mid, rest[0:w, :]))
                    nc.vector.tensor_tensor(lo, rest[0:w, :], mid, ALU.subtract).then_inc(parts_ready, 1)
                elif kind == "v":
                    l, b, i = args
                    full(dve, item)
                    if l:
                        attended(dve, (b + 1) * NG - 1, NT - 1)
                    nc.vector.tensor_copy(V[b][:, 2 * i:2 * i + 2, :, 0:D],
                                          bank[:, 0:2 * C].rearrange("p (t h d) -> p t h d", t=2, h=H)
                                          ).then_inc(bank_free[BANK[item]], 1)
                elif kind == "max":
                    g, u = args
                    j, qt = divmod(u, NT)
                    full(dve, item)
                    if g >= 2 and u == 0:
                        dve.wait_ge(msplit_ready, g - 1)
                    nc.vector.tensor_reduce(negm[:, g % 2, qt, j:j + 1], bank[:, 0:keys_of(g // (B * NG), qt)],
                                            AX.X, ALU.max, negate=True).then_inc(bank_free[BANK[item]], 1)
                elif kind == "o":
                    g, = args
                    l, b, h = lb(g)
                    full(dve, item)
                    if l == 0 and g % NG == 0:
                        for i in ((1,) if b else (0, 2)):
                            dve.wait_ge(low_w[i], 1)
                    if l and g % NG == 0:
                        full(dve, ("aT", l - 1, b, 1))
                    o = bank[:, :].rearrange("p (t j c) -> p t j c", t=NT, j=HG)
                    link(nc.vector.reciprocal(rden[:, :, :], o[:, :, :, D]))
                    nc.vector.tensor_tensor(at[b][:, :, h * D:(h + HG) * D].rearrange("p t (j d) -> p t j d", j=HG),
                                            o[:, :, :, 0:D], rden[:, :, :, None].to_broadcast([P, NT, HG, D]),
                                            ALU.mult).then_inc(bank_free[BANK[item]], 1)
                elif kind in ("proj", "fc2"):
                    l, b, i = args
                    full(dve, item)
                    x = X[b][:, 2 * i:2 * i + 2, :]
                    ins = nc.vector.tensor_tensor(x, x, bank[:, 0:2 * C].rearrange("p (t c) -> p t c", t=2), ALU.add)
                    ins.then_inc(bank_free[BANK[item]], 1)
                elif kind == "fc1":
                    l, b, c = args
                    w = FW[c]
                    released(dve, item)
                    u = U[0:w, c, :]
                    link(nc.vector.tensor_scalar(u, u, 8 * GELU_C * GELU_A, 2 * GELU_C, ALU.mult, ALU.add))
                    nc.vector.tensor_tensor(u, u, xh[0:w, c, :], ALU.mult).then_inc(u_ready, 1)
                elif kind == "gate":
                    l, b, c = args
                    w = FW[c]
                    if l == 0:
                        dve.wait_ge(t_ready, GELU_U[("fc1", l, b, c)])
                    released(dve, ("fc1", l, b, c))
                    u = U[0:w, c, :]
                    nc.vector.scalar_tensor_tensor(u, u, 1.0, xh[0:w, c, :], ALU.add, ALU.mult).then_inc(g_ready, 1)

        @block.tensor
        def _(pe):
            pe.wait_ge(consts, 2)

            def wide_product(bank, w, w_s, c0, n):
                cols = slice(c0, c0 + n)
                nc.tensor.matmul(bank[0:n, :], w[0][:, cols], hT_p[0][:, :], start=True, stop=False)
                nc.tensor.matmul(bank[0:n, :], w[0][:, cols], hT_p[1][:, :], start=False, stop=False)
                nc.tensor.matmul(bank[0:n, :], w[1][:, cols], hT_p[0][:, :], start=False, stop=False)
                return nc.tensor.matmul(bank[0:n, :], w_s[:, cols], hT_s[:, :], start=False, stop=True)

            for item in ORDER["PE"]:
                kind, *args = item
                if item in BEFORE:
                    released(pe, BEFORE[item])
                bank = bank_of(item) if item in BANK else None
                filled_bank = bank_full[BANK[item]] if item in BANK else None
                if kind == "acol":
                    l, k = args
                    pe.wait_ge(silu_ready, 2)
                    pe.wait_ge(ada_in[l][0 if l else k], 48)
                    for r, n in enumerate((P, R)):
                        for s in range(2):
                            cols = slice((3 * k + s) * C + r * P, (3 * k + s) * C + r * P + n)
                            o = bank[0:n, (2 * r + s) * B:(2 * r + s + 1) * B]
                            nc.tensor.matmul(o, w_ada[l][:, cols], cond[:, 3, :], start=True, stop=False)
                            ins = nc.tensor.matmul(o, w_ada_r[l][:, cols], cond_r[:, 3, :], start=False, stop=True)
                    ins.then_inc(filled_bank, 1)
                elif kind == "agate":
                    l, b = args
                    pe.wait_ge(wide_ready, 1)
                    for k in range(2):
                        pe.wait_ge(ada_in[l][0 if l else k], 48)
                        c0 = (3 * k + GA) * C
                        o = bank[:, k * C:(k + 1) * C]
                        nc.tensor.matmul(o, cond_w[:, b, :], w_ada[l][:, c0:c0 + C], start=True, stop=False)
                        ins = nc.tensor.matmul(o, cond_wr[:, b, :], w_ada_r[l][:, c0:c0 + C], start=False, stop=True)
                    ins.then_inc(filled_bank, 1)
                elif kind == "hT":
                    l, b, k, r = args
                    pe.wait_ge(normed, NORM[("norm", l, b, k)])
                    for t in range(NT):
                        src = hn[:, t, P:C] if r else hn[:, t, 0:P]
                        n = R if r else P
                        ins = nc.tensor.transpose(bank[0:n, t * P:(t + 1) * P], src, ident[:, :])
                    ins.then_inc(filled_bank, 1)
                elif kind == "qk":
                    l, b, c = args
                    pe.wait_ge(split, HTN[("hT", l, b, 0, 0)])
                    pe.wait_ge(low_w[2 * l], 1)
                    wide_product(bank, w_qk[l], w_qkv_s[l], c * P, QKW[c]).then_inc(filled_bank, 1)
                elif kind == "v":
                    l, b, i = args
                    for t in range(2):
                        tok = slice((2 * i + t) * P, (2 * i + t + 1) * P)
                        o = bank[:, t * C:(t + 1) * C]
                        nc.tensor.matmul(o, hT[:, tok], w_v[l][:, :], start=True, stop=False)
                        ins = nc.tensor.matmul(o, hT_s[:, tok], w_qkv_s[l][:, QK:3 * C], start=False, stop=True)
                    ins.then_inc(filled_bank, 1)
                elif kind == "max":
                    g, u = args
                    l, b, h = lb(g)
                    j, qt = divmod(u, NT)
                    if u == 0 and g % NG < 2:
                        pe.wait_ge(stacked[g // NG][g % NG], 16 * (NSTACK + (l or g % NG == 0)))
                    w = keys_of(l, qt)
                    o = bank
                    q = QS[b][0:KROWS, h + j, qt * P:(qt + 1) * P]
                    ins = nc.tensor.matmul(o[:, 0:w], q, KS[b][0:KROWS, h + j, 0:w], start=True, stop=(l == 0))
                    if l:
                        ins = nc.tensor.matmul(o[:, w - P:w], identb[:, :], mask_qk[:, :], start=False, stop=True)
                    ins.then_inc(filled_bank, 1)
                elif kind == "mT":
                    g, = args
                    pe.wait_ge(msplit_ready, g + 1)
                    for t in range(NT):
                        ins = nc.tensor.transpose(bank.bitcast(BF16)[0:3 * HG, t * P:(t + 1) * P],
                                                  msp[:, t, :, :].rearrange("p s j -> p (s j)"), identb[:, :])
                    ins.then_inc(filled_bank, 1)
                elif kind == "scores":
                    g, u = args
                    l, b, h = lb(g)
                    kt, j = divmod(u, HG)
                    if u == 0:
                        pe.wait_ge(m_in[g % 2], 16 * (g // 2 + 1))
                    q0 = first_query(l, kt)
                    ins = nc.tensor.matmul(bank[:, q0:T], KS[b][0:KROWS, h + j, kt * P:(kt + 1) * P],
                                           QS[b][0:KROWS, h + j, q0:T], start=True, stop=(l == 0))
                    if l:
                        ins = nc.tensor.matmul(bank[:, q0:q0 + P], identb[:, :], mask_kq[:, :], start=False, stop=True)
                    ins.then_inc(filled_bank, 1)
                elif kind == "pv":
                    g, kt = args
                    l, b, h = lb(g)
                    released(pe, ("scores", g, kt * HG + HG - 1))
                    if kt == 0 and g:
                        pe.wait_ge(o_ready, g)
                    if g == 0 and kt == 0:
                        pe.wait_ge(outputs_filled, 1)
                    if kt == 0 and g % NG == 0:
                        for i in range(2):
                            released(pe, ("v", l, b, i))
                    q0 = first_query(l, kt)
                    for j in range(HG):
                        ins = nc.tensor.matmul(OB[CT * j:CT * j + VW, q0:T], V[b][:, kt, h + j, :],
                                               probs[:, kt % 2, j, q0:T], start=(kt == 0), stop=(kt == NT - 1))
                    ins.then_inc(pv_done, 1)
                elif kind == "o":
                    g, = args
                    pe.wait_ge(o_ready, g + 1)
                    for t in range(NT):
                        ins = nc.tensor.transpose(bank[:, t * P:(t + 1) * P], OT[:, t * P:(t + 1) * P], ident[:, :])
                    ins.then_inc(filled_bank, 1)
                elif kind == "aT":
                    l, b, r = args
                    released(pe, ("o", (l * B + b + 1) * NG - 1))
                    for t in range(NT):
                        src = at[b][:, t, P:C] if r else at[b][:, t, 0:P]
                        n = R if r else P
                        ins = nc.tensor.transpose(bank[0:n, t * P:(t + 1) * P], src, ident[:, :])
                    ins.then_inc(filled_bank, 1)
                elif kind == "proj":
                    l, b, i = args
                    pe.wait_ge(gated, l * B + b + 1)
                    for r in range(2):
                        released(pe, ("aT", l, b, r))
                    for t in range(2):
                        tok = slice((2 * i + t) * P, (2 * i + t + 1) * P)
                        o = bank[:, t * C:(t + 1) * C]
                        nc.tensor.matmul(o, aT[:, tok], g_proj[l][b][:, :], start=True, stop=False)
                        ins = nc.tensor.matmul(o, aT_r[:, tok], g_proj_r[l][b][:, :], start=False, stop=True)
                    ins.then_inc(filled_bank, 1)
                elif kind == "fc1":
                    l, b, c = args
                    pe.wait_ge(split, HTN[("hT", l, b, 1, 0)])
                    pe.wait_ge(low_w[2 * l + 1], 1)
                    wide_product(bank, w_fc1[l], w_fc1_s[l], c * P, FW[c]).then_inc(filled_bank, 1)
                elif kind == "fc2":
                    l, b, i = args
                    pe.wait_ge(g_ready, GATE[("gate", l, b, NF - 1)])
                    pe.wait_ge(filled_late, 1)
                    for t in range(2):
                        tok = slice((2 * i + t) * P, (2 * i + t + 1) * P)
                        for c in range(NF):
                            w = SR if c == NF - 1 else P
                            ins = nc.tensor.matmul(bank[:, t * C:(t + 1) * C], U[0:w, c, tok], g_fc2[l][b][0:w, c, :],
                                                   start=(c == 0), stop=(c == NF - 1))
                    ins.then_inc(filled_bank, 1)


def kernel(**inputs):
    import numpy as np
    from concourse import bacc
    from concourse.bass_utils import run_bass_kernel_spmd

    nc = bacc.Bacc("TRN2", target_bir_lowering=False, num_devices=1)
    arrays, aps = {}, {}
    for name, value in inputs.items():
        v = np.ascontiguousarray(np.asarray(value).T if name == "cond_1152" else value)
        arrays["in_" + name] = v
        aps[name] = nc.dram_tensor("in_" + name, v.shape, mybir.dt.from_np(v.dtype), kind="ExternalInput").ap()
    out = nc.dram_tensor("out", (B, T, C), F32, kind="ExternalOutput").ap()
    two_block_kernel(nc, aps, out)
    r = run_bass_kernel_spmd(nc, [arrays], core_ids=[0])
    return r.results[0]["out"]
```

```python
import concourse.bass as bass
import concourse.mybir as mybir
from contextlib import ExitStack

F32 = mybir.dt.float32
F32R = mybir.dt.float32r
BF16 = mybir.dt.bfloat16
U32 = mybir.dt.uint32
ALU = mybir.AluOpType
ACT = mybir.ActivationFunctionType
AX = mybir.AxisListType

P = 128
B, T, C = 2, 512, 144
L = 2
H = 16
D = C // H
FF = 4 * C
NT = T // P
R = C - P
NG = 4
HG = H // NG
QK = 2 * C
QKW = [128, 128, QK - 256]
FW = [128, 128, 128, 128, FF - 512]
NF = len(FW)
VW = D + 1
CT = 32
SR = 96
EPS = 1e-6
SCALE = float(D) ** -0.5
NEG = -1e30
GELU_C = 0.7978845608028654
GELU_A = 0.044715

Q_RUNS = [(0, 1, 3), (1, 1, 2), (2, 1, 1)]
K_RUNS = [(0, 3, 1), (0, 2, 1), (0, 1, 1)]
PRODUCTS = 6
MROW = PRODUCTS * D
KROWS = 96

SH, SC, GA = 0, 1, 2


def tiles(s):
    return ((0, NT), (0, NT // 2), (NT // 2, NT))[s]


def part_with(l, b, i):
    return i + 1 if (l, b) == (L - 1, B - 1) else 0


def head_items(l, b):
    return ([("stats", l, b, 0, 0), ("norm", l, b, 0, 0), ("hT", l, b, 0, 1, 0), ("hT", l, b, 0, 0, 0)]
            + [("qk", l, b, c) for c in (2, 0, 1)] + [("v", l, b, i) for i in range(2)])


def mlp_items(l, b, s):
    items = []
    for c in range(NF + 2):
        if c < NF:
            items.append(("fc1", l, b, c, s))
        if c >= 1 and c - 1 < NF:
            items.append(("tanh", l, b, c - 1, s))
        if c >= 2:
            items.append(("gate", l, b, c - 2, s))
    return items


def tail_items(l, b):
    if part_with(l, b, 0) == 0:
        return ([("aT", l, b, r, 0) for r in range(2)] + [("proj", l, b, i) for i in range(2)]
                + [("stats", l, b, 1, 0), ("norm", l, b, 1, 0), ("hT", l, b, 1, 1, 0), ("hT", l, b, 1, 0, 0)]
                + mlp_items(l, b, 0) + [("fc2", l, b, i) for i in range(2)])
    items = [("aT", l, b, r, s) for s in (1, 2) for r in range(2)]
    items += [("proj", l, b, 0), ("stats", l, b, 1, 1), ("proj", l, b, 1), ("norm", l, b, 1, 1), ("stats", l, b, 1, 2),
              ("hT", l, b, 1, 1, 1), ("hT", l, b, 1, 0, 1), ("norm", l, b, 1, 2), ("hT", l, b, 1, 1, 2), ("hT", l, b, 1, 0, 2)]
    return items + mlp_items(l, b, 1) + mlp_items(l, b, 2) + [("fc2", l, b, i) for i in range(2)]


SIDE = ([("stats", 0, 0, 0, 0), ("acol", 0, 0), ("norm", 0, 0, 0, 0), ("wsplit", 0, 0)] + head_items(0, 0)[2:4]
        + head_items(0, 1)[:1] + head_items(0, 0)[4:] + head_items(0, 1)[1:]
        + tail_items(0, 0) + head_items(1, 0) + tail_items(0, 1) + head_items(1, 1)
        + tail_items(1, 0) + tail_items(1, 1))
WEIGHTS = ([("acol", 0, 1), ("wsplit", 0, 1), ("wsplit", 1, 0), ("wsplit", 1, 1), ("acol", 1, 0), ("acol", 1, 1)]
           + [("agate", l, b) for l in range(L) for b in range(B)])
GROUPS = L * B * NG
BANKS = 7


def keys_of(l, qt):
    return (qt + 1) * P if l else T


def first_query(l, kt):
    return kt * P if l else 0


def steps():
    out = []

    def add(stream, engine, item, ns, *after):
        out.append((stream, engine, item, ns, after))

    cost = {"acol": (950, 350), "agate": (980, 370), "v": (660, 370), "proj": (980, 370), "fc2": (2460, 370)}
    loaded = {("acol", 0, 0): 5500, ("wsplit", 0, 0): 7500, ("wsplit", 0, 1): 15500, ("stats", 0, 0, 0, 0): 4500,
              ("stats", 0, 1, 0, 0): 9500,
              ("acol", 0, 1): 36000, ("agate", 0, 0): 60000}
    norm = None
    for item in SIDE + WEIGHTS:
        kind, l, *rest = item
        b = rest[0]
        size = 0.5 if kind in ("stats", "norm", "hT", "aT", "fc1", "tanh", "gate") and rest[-1] else 1
        stream = "side" if item in SIDE else "weights"
        if kind in cost:
            after = {"acol": [], "agate": [],
                     "v": [("DVE", ("hT", l, b, 0, 0, 0))],
                     "proj": [*(("ACT", ("aT", l, b, r, part_with(l, b, rest[-1]))) for r in range(2)), ("POOL", ("agate", l, b))],
                     "fc2": [("DVE", ("gate", l, b, NF - 1, part_with(l, b, rest[-1])))]}[kind]
            add(stream, "PE", item, cost[kind][0], *after, loaded.get(item, 0))
            add(stream, "DVE", item, cost[kind][1], ("PE", item))
            if kind == "agate":
                add(stream, "POOL", item, 3200, ("DVE", item), 66000)
            if kind == "fc2" and l == L - 1:
                add("side", "SP", item, 500, ("DVE", item))
        elif kind == "wsplit":
            add(stream, "ACT", item, 1700, loaded.get(item, 0))
            if stream == "side":
                add(stream, "DVE", item, 1100, ("ACT", item))
            else:
                add(stream, "POOL", item, 6500 if b else 3500, ("ACT", item), 19000)
        elif kind == "stats":
            k, t0, t1 = rest[1], *tiles(rest[2])
            last = ("proj", l, b) if k else ("fc2", l - 1, b)
            add("side", "DVE", item, 1500 * size + 200, loaded.get(item, 0),
                *([("DVE", (*last, i)) for i in range(t0 // 2, t1 // 2)] if l or k else []))
            add("side", "POOL", item, 960, ("DVE", item), 0 if l or k or not b else 18500)
        elif kind == "norm":
            after = [("POOL", ("stats", *item[1:]))]
            if norm and norm != item[:4]:
                after += [("PE", ("hT", *norm[1:], r, 0)) for r in range(2)]
            norm = item[:4]
            add("side", "DVE", item, 1060 * size, *after)
        elif kind == "hT":
            k, r, _ = rest[1:]
            add("side", "PE", item, 430 * size, ("DVE", ("norm", l, b, k, rest[-1])))
            add("side", "ACT", item, (600 * size + 60), ("PE", item), ("DVE", ("acol", l, k)))
            add("side", "DVE", item, (1400 if r else 1070) * size + 2100 * (item[1:] == (0, 0, 0, 0, 0)), ("ACT", item))
        elif kind == "qk":
            add("side", "PE", item, 860, ("DVE", ("hT", l, b, 0, 0, 0)), ("POOL", ("wsplit", l, 0)) if l else ("DVE", ("wsplit", 0, 0)))
            c = rest[1]
            add("side", "ACT", item, 4000 if (l, b, c) == (0, 0, 1) else 480, ("PE", item))
            add("side", "DVE", item, 1700, ("ACT", item))
            after = [("PE", ("scores", (b + 1) * NG - 1, 15))] if l and c < 2 else []
            add("side", "SP", item, (500, 6700, 1000)[c], ("DVE", item), *after)
        elif kind == "aT":
            add("side", "PE", item, 430 * size, ("DVE", ("o", (l * B + b + 1) * NG - 1)))
            add("side", "ACT", item, (420 * size + 60), ("PE", item))
        elif kind == "fc1":
            c = rest[1]
            mlp = ([("DVE", ("gate", *((l, 0) if b else (l - 1, 1)), c, 0))] if l or b else
                   [("POOL", ("wsplit", 1, 1)), ("PE", ("agate", 1, B - 1))])
            add("side", "PE", item, 860 * size, ("DVE", ("hT", l, b, 1, 0, rest[-1])), ("POOL", ("wsplit", l, 1)))
            add("side", "ACT", item, 960 * size, ("PE", item), *mlp)
            if l == 0:
                add("side", "DVE", item, 620 * size, ("ACT", item))
        elif kind == "tanh" and l == 0:
            add("side", "ACT", item, 520 * size, ("DVE", ("fc1", *item[1:])))
        elif kind == "gate":
            add("side", "DVE", item, 620 * size, ("ACT", ("fc1" if l else "tanh", *item[1:])))
    for g in range(GROUPS):
        l, b = g // (B * NG), g // NG % B
        for u in range(HG * NT):
            w = keys_of(l, u % NT)
            add("max", "PE", ("max", g, u), w / 2.4 + 60 * l, ("SP", ("qk", l, b, 1)))
            add("max", "DVE", ("max", g, u), w / 0.96 + 65, ("PE", ("max", g, u)),
                *([("POOL", ("msplit", g - 2))] if g >= 2 else []))
        add("shift", "POOL", ("msplit", g), 1000, ("DVE", ("max", g, 15)), *([("PE", ("mT", g - 1))] if g else []))
        add("shift", "PE", ("mT", g), 250, ("POOL", ("msplit", g)))
        add("shift", "ACT", ("mT", g), 480, ("PE", ("mT", g)))
        add("rows", "POOL", ("mT", g), 1000, ("ACT", ("mT", g)))
        for u in range(HG * NT):
            kt = u // HG
            w = T - first_query(l, kt)
            n = g * NT + kt
            add("attend", "PE", ("scores", g, u), w / 2.4 + 60 * l, ("rows", ("mT", g)))
            add("attend", "ACT", ("scores", g, u), w / 1.2 + 60, ("PE", ("scores", g, u)),
                *([("PE", ("pv", (n - 2) // NT, (n - 2) % NT))] if n >= 2 else []))
            if u % HG == HG - 1:
                add("gather", "PE", ("pv", g, kt), w * 1.67 + 60, ("ACT", ("scores", g, u)),
                    *([("ACT", ("oT", g - 1))] if g and kt == 0 else []))
        add("gather", "ACT", ("oT", g), 480, ("PE", ("pv", g, NT - 1)), *([("PE", ("o", g - 1))] if g else []))
        add("gather", "PE", ("o", g), 450, ("ACT", ("oT", g)))
        add("gather", "DVE", ("o", g), 500, ("PE", ("o", g)))
    return out


READER = {"hT": "ACT", "qk": "DVE", "fc1": "ACT", "aT": "ACT", "mT": "ACT", "scores": "ACT"}
ENGINES = ("PE", "ACT", "DVE", "POOL", "SP")
HOLD = {"attend": 4, "max": 4, "shift": 2}
OTHERS, CALM = 2, 5
HASTE = {"head": (20000, 80000, 20000, 20000), "tail": (20000, 80000, 0, 20000), "gather": (0, 0, 0, 10000), "shift": (10000, 20000, 2000, 3000), "max": (-3000, 0, 20000, 0)}
HANDOVER = 160
WINDOW = 0


def haste(stream, item):
    if stream == "side":
        heads = item[0] in ("stats", "norm", "hT") and item[3] == 0 or item[0] in ("qk", "v")
        return HASTE["head" if heads else "tail"][item[1] * B + item[2]]
    return HASTE[stream][item[1] // NG] if stream in HASTE else 0


def plan():
    queues, cost, after, behind, inf = {}, {}, {}, {}, float("inf")
    for stream, engine, item, ns, follows in steps():
        queue = queues.setdefault((engine, stream), [])
        cost[engine, item], after[engine, item] = ns, follows
        for follow in [*follows, *((engine, last) for last in queue[-1:])]:
            if not isinstance(follow, int):
                behind.setdefault(("POOL", follow[1]) if follow[0] == "rows" else follow, []).append((engine, item))
        queue.append(item)
    urgency = {}

    def chain_from(step):
        stack = [step]
        while stack:
            top = stack[-1]
            open_ones = [x for x in behind.get(top, []) if x not in urgency]
            if open_ones:
                stack.extend(open_ones)
            else:
                urgency[top] = cost[top] + max([urgency[x] for x in behind.get(top, [])], default=0)
                stack.pop()

    for step in cost:
        if step not in urgency:
            chain_from(step)
    at = {q: 0 for q in queues}
    free = {engine: 0 for engine in ENGINES}
    done, order = {}, {engine: [] for engine in ENGINES}
    bank, before, holder = {}, {}, [(None, None)] * BANKS
    while any(at[q] < len(items) for q, items in queues.items()):
        best = None
        for engine in ENGINES:
            mine_best = []
            for q in queues:
                stream = q[1]
                if q[0] != engine or at[q] == len(queues[q]):
                    continue
                item = queues[q][at[q]]
                ends = []
                for follow in after[engine, item]:
                    if isinstance(follow, int):
                        ends.append(follow)
                    elif follow[0] == "rows":
                        ends.append(done.get(("POOL", follow[1]), inf) + 2000 + HANDOVER)
                    else:
                        ends.append(done.get(follow, inf) + HANDOVER)
                start = max([free[engine], *ends])
                if start == inf:
                    continue
                k = None
                if engine == "PE" and item[0] != "pv":
                    left = [None if i is None else done.get((READER.get(i[0], "DVE"), i)) for i, _ in holder]
                    holds = [s == stream and i is not None and (t is None or t > start)
                             for (i, s), t in zip(holder, left)]
                    group = stream if stream in HOLD else "other"
                    others = [s not in HOLD and i is not None and (t is None or t > start)
                              for (i, s), t in zip(holder, left)]
                    calm = at["PE", "max"] == 0 or at["PE", "attend"] == len(queues["PE", "attend"])
                    used = sum(others) if group == "other" else sum(holds)
                    if used >= HOLD.get(group, CALM if calm else OTHERS):
                        mine = [t for h, t in zip(others if group == "other" else holds, left) if h and t is not None]
                        if not mine:
                            continue
                        start = max(start, min(mine) + HANDOVER)
                    ready = [(0 if i is None else t, n) for n, ((i, _), t) in enumerate(zip(holder, left))
                             if i is None or t is not None]
                    if not ready:
                        continue
                    t, k = min(ready)
                    start = max(start, t + HANDOVER if holder[k][0] else 0)
                mine_best.append((start, -urgency[engine, item] - haste(stream, item), engine, stream, item, k))
            if mine_best:
                first = min(mine_best)[0]
                chosen = min((c for c in mine_best if c[0] <= first + WINDOW), key=lambda c: c[1])
                if best is None or chosen[0] < best[0]:
                    best = chosen
        start, _, engine, stream, item, k = best
        at[engine, stream] += 1
        free[engine] = done[engine, item] = start + cost[engine, item]
        order[engine].append(item)
        if k is not None:
            bank[item] = k
            if holder[k][0]:
                before[item] = holder[k][0]
            holder[k] = (item, stream)
    return order, bank, before


ORDER, BANK, BEFORE = plan()


def ordinals(kinds):
    return {item: n for n, item in enumerate((item for item in SIDE if item[0] in kinds), 1)}


def two_block_kernel(nc, a, out):
    ctx = ExitStack()

    def sb(name, shape, dt=F32):
        return ctx.enter_context(nc.sbuf_tensor(name, shape, dt))

    def ps(name, shape):
        return ctx.enter_context(nc.psum_tensor(name, shape, F32))

    def sem(name):
        return ctx.enter_context(nc.semaphore(name))

    with ctx:
        ident = sb("ident", [P, P])
        identb = sb("identb", [P, P], BF16)
        mask_qk = sb("mask_qk", [P, P], BF16)
        mask_kq = sb("mask_kq", [P, P], BF16)
        onesb = sb("onesb", [P, T], BF16)
        zerosb = sb("zerosb", [P, T], BF16)
        w_qk = [[sb(f"w_qk{l}{i}", [P, QK], F32R) for i in range(2)] for l in range(L)]
        w_v = [sb(f"w_v{l}", [P, C]) for l in range(L)]
        w_qkv_s = [sb(f"w_qkv_s{l}", [SR, 3 * C], F32R) for l in range(L)]
        w_fc1 = [[sb(f"w_fc1{l}{i}", [P, FF], F32R) for i in range(2)] for l in range(L)]
        w_fc1_s = [sb(f"w_fc1_s{l}", [SR, FF], F32R) for l in range(L)]
        w_proj = [sb(f"w_proj{l}", [P, C]) for l in range(L)]
        w_proj_r = [sb(f"w_proj_r{l}", [R + 1, C]) for l in range(L)]
        w_fc2 = [sb(f"w_fc2{l}", [P, NF, C]) for l in range(L)]
        g_proj = [[sb(f"g_proj{l}{b}", [P, C]) for b in range(B)] for l in range(L)]
        g_proj_r = [[sb(f"g_proj_r{l}{b}", [SR, C]) for b in range(B)] for l in range(L)]
        g_fc2 = [[sb(f"g_fc2{l}{b}", [P, NF, C]) for b in range(B)] for l in range(L)]
        cond = sb("cond", [P, 4, B])
        cond_r = sb("cond_r", [R + 1, 4, B])
        cond_w = sb("cond_w", [P, B, P])
        cond_wr = sb("cond_wr", [R + 1, B, P])
        mod = [sb(f"mod{l}", [P, 2, 2, B]) for l in range(L)]
        mod_r = [sb(f"mod_r{l}", [R, 2, 2, B]) for l in range(L)]
        X = [sb(f"X{b}", [P, NT, C]) for b in range(B)]
        stat = sb("stat", [P, NT, 6])
        mean = sb("mean", [P, NT, 2])
        veps = sb("veps", [P, NT])
        rstd = sb("rstd", [P, NT])
        half = sb("half", [P, NT])
        hn = sb("hn", [P, NT, C])
        hT = sb("hT", [P, T])
        hT_p = [sb(f"hT_p{i}", [P, T], F32R) for i in range(2)]
        hT_r = sb("hT_r", [R, T])
        hT_s = sb("hT_s", [SR, T], F32R)
        parts = sb("parts", [P, 3, 3, T], BF16)
        rest = sb("rest", [P, T])
        QS = [sb(f"QS{b}", [P, H, T], BF16) for b in range(B)]
        KS = [sb(f"KS{b}", [P, H, T], BF16) for b in range(B)]
        gates = [[sb(f"gates{l}{b}", [P, 2, C]) for b in range(B)] for l in range(L)]
        V = [sb(f"V{b}", [P, NT, H, VW]) for b in range(B)]
        probs = sb("probs", [P, 2, HG, T])
        negm = sb("negm", [P, 2, NT, HG])
        mrest = sb("mrest", [P, NT, HG])
        msp = sb("msp", [P, NT, 3, HG], BF16)
        mT = sb("mT", [3 * HG, 2, T], BF16)
        OT = sb("OT", [P, T])
        rden = sb("rden", [P, NT, HG])
        at = [sb(f"at{b}", [P, NT, C]) for b in range(B)]
        aT = sb("aT", [P, T])
        aT_r = sb("aT_r", [SR, T])
        xh = sb("xh", [P, NF, T])
        U = sb("U", [P, NF, T])
        ada_cols = L * 6 * C
        flat_xh, flat_U = (t[:, :, :].rearrange("p c t -> p (c t)") for t in (xh, U))
        w_ada = [flat_xh[:, l * 6 * C:(l + 1) * 6 * C] for l in range(L)]
        w_ada_r = [flat_U[0:R + 1, l * 6 * C:(l + 1) * 6 * C] for l in range(L)]
        flat_at = [t[:, :, :].rearrange("p t c -> p (t c)") for t in at]
        raw = [[flat_at[0][:, 0:QK], flat_at[1][:, :]],
               [flat_at[0][:, QK:2 * QK], flat_xh[:, ada_cols:ada_cols + FF]]]
        raw_r = [[(aT[0:R + 1, 0:3 * C], OT[0:R + 1, 0:3 * C])[l],
                  g_fc2[1][l][0:R + 1, :, :].rearrange("p c n -> p (c n)")[:, 0:FF]] for l in range(L)]

        PB = [ps(f"PB{k}", [P, T]) for k in range(BANKS)]
        OB = ps("OB", [P, T])

        def bank_of(item):
            return PB[BANK[item]][:, :]

        scratch = nc.dram_tensor("qk_parts", [L, B, 2, 3, D, H, T], BF16, kind="Internal").ap()

        cond_in = sem("cond_in")
        ada_in = [[sem(f"ada_in{l}{k}") for k in range(2 - l)] for l in range(L)]
        x_in = [sem(f"x_in{b}") for b in range(B)]
        qkv_in = [sem(f"qkv_in{l}") for l in range(L)]
        proj_in = [sem(f"proj_in{l}") for l in range(L)]
        fc1_in = [sem(f"fc1_in{l}") for l in range(L)]
        rows_zero = sem("rows_zero")
        filled_first = sem("filled_first")
        filled = sem("filled")
        q_zeroed = [sem(f"q_zeroed{b}") for b in range(B)]
        k_zeroed = [sem(f"k_zeroed{b}") for b in range(B)]
        filled_late = sem("filled_late")
        consts = sem("consts")
        pool_step = sem("pool_step")
        dve_step = sem("dve_step")
        th_ready = sem("th_ready")
        silu_ready = sem("silu_ready")
        high_w = sem("high_w")
        low_w = [sem(f"low_w{l}{k}") for l in range(L) for k in range(2)]
        wide_ready = sem("wide_ready")
        split = sem("split")
        gw_filled = sem("gw_filled")
        gated = sem("gated")
        outputs_filled = sem("outputs_filled")
        stats_ready = sem("stats_ready")
        rstd_ready = sem("rstd_ready")
        normed = sem("normed")
        bank_full = [sem(f"bank_full{k}") for k in range(BANKS)]
        bank_free = [sem(f"bank_free{k}") for k in range(BANKS)]
        high_ready = sem("high_ready")
        parts_ready = sem("parts_ready")
        parts_out = [sem(f"parts_out{i}") for i in range(2)]
        stacked = [[sem(f"stacked{p}{i}") for i in range(2)] for p in range(L * B)]
        msplit_ready = sem("msplit_ready")
        m_in = [sem(f"m_in{i}") for i in range(2)]
        pv_done = sem("pv_done")
        o_ready = sem("o_ready")
        u_ready = sem("u_ready")
        t_ready = sem("t_ready")
        g_ready = sem("g_ready")
        stored = sem("stored")

        nth = {}
        for k in range(BANKS):
            for n, i in enumerate((i for i in ORDER["PE"] if BANK.get(i) == k), 1):
                nth[i] = n
        STATS = ordinals(("stats",))
        NORM = ordinals(("norm",))
        QKN = ordinals(("qk",))
        GATE = ordinals(("gate",))
        HTN = ordinals(("hT",))
        GELU_U = {i: n for n, i in enumerate((i for i in SIDE if i[0] == "fc1" and i[1] == 0), 1)}
        NSTACK = len(Q_RUNS) + len(K_RUNS)

        def full(eng, item):
            eng.wait_ge(bank_full[BANK[item]], nth[item])

        def released(eng, item):
            eng.wait_ge(bank_free[BANK[item]], nth[item])

        def attended(eng, g, kt):
            eng.wait_ge(pv_done, g * NT + kt + 1)

        def tokens(s):
            t0, t1 = tiles(s)
            return slice(t0 * P, t1 * P)

        def before(l, b):
            return (l, 0) if b else (l - 1, 1)

        def lb(g):
            return g // (B * NG), g // NG % B, g % NG * HG

        def by_part(w):
            v = w.rearrange("p (s h d) -> p s d h", s=2, h=H)
            return v[:, :, 0:D - 1, :], v[:, :, D - 1, :]

        def in_part(w):
            return (w[:, 0:2 * P].rearrange("p (s d h) -> p s d h", s=2, h=H),
                    w[:, 2 * P:QK].rearrange("p (s h) -> p s h", s=2))

        def pieces(l, k):
            n = R + 1
            if k:
                s, r = w_fc1_s[l], raw_r[l][1]
                return [(raw[l][1], w_fc1[l][0][:, :], w_fc1[l][1][:, :]), (r, s[0:n, :], s[64:64 + n, :])]
            s, r = w_qkv_s[l], raw_r[l][0]
            out = [*zip(by_part(raw[l][0]), in_part(w_qk[l][0][:, :]), in_part(w_qk[l][1][:, :]))]
            out += [*zip(by_part(r[:, 0:QK]), in_part(s[0:n, 0:QK]), in_part(s[64:64 + n, 0:QK]))]
            return out + [(r[:, QK:], s[0:n, QK:], s[64:64 + n, QK:])]

        def low_values(eng, l, k, link):
            for n, (whole, high, low) in enumerate(pieces(l, k), 1):
                ins = eng.tensor_tensor(low, whole, high.bitcast(F32), ALU.subtract)
                if n < len(pieces(l, k)):
                    link(ins)
            return ins

        block = ctx.enter_context(nc.Block())

        @block.sync
        def _(sp):
            sp.dma_start(cond[:, 0, :], a["cond_1152"][0:P]).then_inc(cond_in, 16)
            sp.dma_start(cond_r[0:R, 0, :], a["cond_1152"][P:C]).then_inc(cond_in, 16)
            row = lambda v: v.rearrange("(a n) -> a n", a=1)
            ada = [("L0_cond_W_ada", "L0_cond_b_ada"), ("L1_cond_Wa", "L1_cond_ba")]
            qkv = [[("L0_cond_W_qkv", i * C) for i in range(3)], [("L1_cond_Wq", 0), ("L1_cond_Wk", 0), ("L1_cond_Wv", 0)]]

            def load_ada(l, k, n=1):
                w, bias = (a[name] for name in ada[l])
                cols = slice(k * 3 * C, (k + n) * 3 * C)
                sp.dma_start(w_ada[l][:, cols], w[0:P, cols]).then_inc(ada_in[l][k], 16)
                sp.dma_start(w_ada_r[l][0:R, cols], w[P:C, cols]).then_inc(ada_in[l][k], 16)
                sp.dma_start(w_ada_r[l][R:R + 1, cols], row(bias)[:, cols]).then_inc(ada_in[l][k], 16)

            def load_x(b):
                sp.dma_start(X[b][:, :, :], a["x"][b].rearrange("(t p) c -> p t c", p=P)).then_inc(x_in[b], 16)

            load_x(0)
            load_ada(0, 0)
            w = a["L0_cond_W_qkv"]
            sp.dma_start(raw[0][0], w[0:P, 0:QK]).then_inc(qkv_in[0], 16)
            sp.dma_start(raw_r[0][0][0:R], w[P:C, :]).then_inc(qkv_in[0], 16)
            sp.dma_start(raw_r[0][0][R:R + 1], row(a["L0_cond_b_qkv"])).then_inc(qkv_in[0], 16)
            sp.dma_start(w_v[0][:, :], w[0:P, QK:3 * C]).then_inc(qkv_in[0], 16)
            load_ada(0, 1)
            load_x(1)
            sp.wait_ge(filled, 1)
            names = [("L0_cond_W_proj", "L0_cond_b_proj", "L0_cond_W_fc1", "L0_cond_b_fc1",
                      "L0_cond_W_fc2", "L0_cond_b_fc2"),
                     ("L1_cond_Wp", "L1_cond_bp", "L1_cond_W1", "L1_cond_b1", "L1_cond_W2", "L1_cond_b2")]

            def load_fc1(l):
                w1, b1 = (a[n] for n in names[l][2:4])
                sp.dma_start(raw[l][1], w1[0:P, :]).then_inc(fc1_in[l], 16)
                sp.dma_start(raw_r[l][1][0:R], w1[P:C, :]).then_inc(fc1_in[l], 16)
                sp.dma_start(raw_r[l][1][R:R + 1], row(b1)).then_inc(fc1_in[l], 16)

            def load_out(l):
                wp, bp, _, _, w2, b2 = (a[n] for n in names[l])
                sp.dma_start(w_proj[l][:, :], wp[0:P, :]).then_inc(proj_in[l], 16)
                sp.dma_start(w_proj_r[l][0:R], wp[P:C, :]).then_inc(proj_in[l], 16)
                sp.dma_start(w_proj_r[l][R:R + 1], row(bp)).then_inc(proj_in[l], 16)
                sp.dma_start(w_fc2[l][:, 0:4, :], w2[0:4 * P, :].rearrange("(c p) n -> p c n", p=P)).then_inc(proj_in[l], 16)
                sp.dma_start(w_fc2[l][0:FW[4], 4, :], w2[4 * P:FF, :]).then_inc(proj_in[l], 16)
                sp.dma_start(w_fc2[l][FW[4]:FW[4] + 1, 4, :], row(b2)).then_inc(proj_in[l], 16)

            def load_rest(part):
                if part == 0:
                    load_fc1(0)
                    for i, name in enumerate(("L1_cond_Wq", "L1_cond_Wk")):
                        sp.dma_start(raw[1][0][:, i * C:(i + 1) * C], a[name][0:P, :]).then_inc(qkv_in[1], 16)
                    for i, name in enumerate(("L1_cond_Wq", "L1_cond_Wk", "L1_cond_Wv")):
                        sp.dma_start(raw_r[1][0][0:R, i * C:(i + 1) * C], a[name][P:C, :]).then_inc(qkv_in[1], 16)
                    sp.dma_start(w_v[1][:, :], a["L1_cond_Wv"][0:P, :]).then_inc(qkv_in[1], 16)
                    load_fc1(1)
                    load_ada(1, 0, 2)
                else:
                    load_out(0)
                    load_out(1)

            load_rest(0)

            for item in ORDER["SP"]:
                kind, *args = item
                if kind == "qk":
                    l, b, c = args
                    sp.wait_ge(parts_ready, QKN[item])
                    if c == 2:
                        for i in range(2):
                            sp.dma_start(scratch[l, b, i, :, D - 1].rearrange("s h t -> h s t"),
                                         parts[i * H:(i + 1) * H, 2, :, :]).then_inc(parts_out[i], 16)
                        if l == 0:
                            sp.wait_ge(k_zeroed[b], 1)
                            sp.wait_ge(rows_zero, 1)
                            sp.dma_start(KS[b][MROW:MROW + 3, :, :],
                                         onesb[0:3, None, :].to_broadcast([3, H, T])).then_inc(stacked[b][0], 16)
                        continue
                    sp.dma_start(scratch[l, b, c, :, 0:D - 1].rearrange("s d h t -> (d h) s t"),
                                 parts[:, c, :, :]).then_inc(parts_out[c], 16)
                    if c == 0:
                        continue
                    if l:
                        full(sp, ("scores", (b + 1) * NG - 1, HG * NT - 1))
                        sp.wait_ge(rows_zero, 2)
                        sp.dma_start(QS[b][MROW:MROW + 3, :, :],
                                     zerosb[0:3, None, :].to_broadcast([3, H, T])).then_inc(stacked[l * B + b][0], 16)
                    else:
                        sp.wait_ge(q_zeroed[b], 1)
                    for i, (h0, h1) in enumerate(((0, HG), (HG, H))):
                        for dst, which, runs in ((QS[b], 0, Q_RUNS), (KS[b], 1, K_RUNS)):
                            sp.wait_ge(parts_out[which], 32 * (l * B + b + 1))
                            row0 = 0
                            for first, n, times in runs:
                                src = scratch[l, b, which, first:first + n, :, h0:h1, :]
                                if times > 1:
                                    src = src.to_broadcast([times, D, h1 - h0, T])
                                rows = D * n * times
                                sp.dma_start(dst[row0:row0 + rows, h0:h1, :], src).then_inc(stacked[l * B + b][i], 16)
                                row0 += rows
                    if (l, b) == (0, 0):
                        load_rest(1)
                elif kind == "fc2":
                    l, b, i = args
                    released(sp, item)
                    sp.dma_start(out[b, 2 * i * P:2 * (i + 1) * P, :].rearrange("(t p) c -> p t c", p=P),
                                 X[b][:, 2 * i:2 * i + 2, :]).then_inc(stored, 16)
            sp.wait_ge(stored, 16 * 2 * B)

        @block.gpsimd
        def _(pool):
            chain = [0]

            def link(ins):
                chain[0] += 1
                ins.then_inc(pool_step, 1)
                pool.wait_ge(pool_step, chain[0])

            nc.gpsimd.memset(ident[:, :], 0.0)
            nc.gpsimd.memset(identb[:, :], 0.0)
            nc.gpsimd.memset(mask_qk[:, :], 0.0)
            link(nc.gpsimd.memset(mask_kq[:, :], 0.0))
            nc.gpsimd.affine_select(out=ident[:, :], in_=ident[:, :], compare_op=ALU.not_equal, fill=1.0,
                                    base=0, pattern=[[-1, P]], channel_multiplier=1)
            nc.gpsimd.affine_select(out=identb[:, :], in_=identb[:, :], compare_op=ALU.not_equal, fill=1.0,
                                    base=0, pattern=[[-1, P]], channel_multiplier=1)
            nc.gpsimd.memset(half[:, :], -0.5).then_inc(consts, 1)
            nc.gpsimd.affine_select(out=mask_qk[:, :], in_=mask_qk[:, :], compare_op=ALU.is_ge, fill=NEG,
                                    base=0, pattern=[[-1, P]], channel_multiplier=1)
            nc.gpsimd.affine_select(out=mask_kq[:, :], in_=mask_kq[:, :], compare_op=ALU.is_ge, fill=NEG,
                                    base=0, pattern=[[1, P]], channel_multiplier=-1).then_inc(consts, 1)

            nc.gpsimd.memset(raw_r[1][0], 0.0)
            nc.gpsimd.memset(w_qkv_s[1][:, :].bitcast(F32), 0.0)
            for l in range(L):
                ins = nc.gpsimd.memset(w_fc1_s[l][:, :].bitcast(F32), 0.0)
            ins.then_inc(filled, 1)
            nc.gpsimd.memset(onesb[0:3, :], 1.0).then_inc(rows_zero, 1)
            nc.gpsimd.memset(zerosb[:, :], 0.0).then_inc(rows_zero, 1)

            def gate_weights(l, b):
                released(pool, ("agate", l, b))
                pool.wait_ge(proj_in[l], 16 * 6)
                pool.wait_ge(gw_filled, 1)
                g = gates[l][b]
                nc.gpsimd.tensor_tensor(g_proj[l][b][:, :], w_proj[l][:, :], g[:, 0, :], ALU.mult)
                nc.gpsimd.tensor_tensor(g_proj_r[l][b][0:R + 1, :], w_proj_r[l][:, :], g[0:R + 1, 0, :], ALU.mult)
                for c in range(NF):
                    w = FW[c] + (c == NF - 1)
                    last = nc.gpsimd.tensor_tensor(g_fc2[l][b][0:w, c, :], w_fc2[l][0:w, c, :], g[0:w, 1, :], ALU.mult)
                last.then_inc(gated, 1)

            for item in ORDER["POOL"]:
                kind, *args = item
                if kind == "stats":
                    l, b, k, s = args
                    t0, t1 = tiles(s)
                    pool.wait_ge(stats_ready, STATS[item])
                    if STATS[item] == 1:
                        pool.wait_ge(consts, 1)
                    nc.gpsimd.tensor_tensor(rstd[:, t0:t1], veps[:, t0:t1], half[:, t0:t1], ALU.pow).then_inc(rstd_ready, 1)
                    if STATS[item] == 1:
                        nc.gpsimd.memset(KS[0][0:KROWS, :, :].bitcast(U32), 0).then_inc(k_zeroed[0], 1)
                        nc.gpsimd.memset(QS[0][0:KROWS, :, :].bitcast(U32), 0).then_inc(q_zeroed[0], 1)
                        nc.gpsimd.memset(KS[1][0:KROWS, :, :].bitcast(U32), 0).then_inc(k_zeroed[1], 1)
                        for i in range(L):
                            for j in range(B):
                                ins = nc.gpsimd.memset(g_proj_r[i][j][:, :], 0.0)
                        link(ins)
                        for i in range(L):
                            for j in range(B):
                                ins = nc.gpsimd.memset(g_fc2[i][j][64:SR, NF - 1, :], 0.0)
                        ins.then_inc(gw_filled, 1)
                        nc.gpsimd.memset(U[64:SR, NF - 1, :], 1.0).then_inc(filled_late, 1)
                        pool.wait_ge(filled_late, 1)
                elif kind == "wsplit":
                    l, k = args
                    pool.wait_ge(high_w, 2 * l + k + 1)
                    low_values(nc.gpsimd, l, k, link).then_inc(low_w[2 * l + k], 1)
                    pool.wait_ge(low_w[2 * l + k], 1)
                elif kind == "agate":
                    gate_weights(*args)
                elif kind == "msplit":
                    g, = args
                    released(pool, ("max", g, HG * NT - 1))
                    if g:
                        full(pool, ("mT", g - 1))
                    m = negm[:, g % 2, :, :]
                    link(nc.gpsimd.tensor_copy(msp[:, :, 0, :], m))
                    link(nc.gpsimd.tensor_tensor(mrest[:, :, :], m, msp[:, :, 0, :], ALU.subtract))
                    link(nc.gpsimd.tensor_copy(msp[:, :, 1, :], mrest[:, :, :]))
                    nc.gpsimd.tensor_tensor(msp[:, :, 2, :], mrest[:, :, :], msp[:, :, 1, :],
                                            ALU.subtract).then_inc(msplit_ready, 1)
                elif kind == "mT":
                    g, = args
                    l, b, h = lb(g)
                    released(pool, item)
                    pool.dma_start(QS[b][MROW:MROW + 3, h:h + HG, :], mT[:, g % 2, :]).then_inc(m_in[g % 2], 16)

        @block.scalar
        def _(act):
            act.wait_ge(silu_ready, 1)
            nc.scalar.activation(cond[:, 2, :], cond[:, 1, :], ACT.Tanh)
            nc.scalar.activation(cond_r[0:R, 2, :], cond_r[0:R, 1, :], ACT.Tanh).then_inc(th_ready, 1)
            for item in ORDER["ACT"]:
                kind, *args = item
                if kind == "wsplit":
                    l, k = args
                    act.wait_ge(fc1_in[l] if k else qkv_in[l], 48 if k else (96 if l else 64))
                    act.wait_ge(filled if l or k else filled_first, 1)
                    for whole, high, low in pieces(l, k):
                        nc.scalar.activation(high, whole, ACT.Copy)
                    r, s = raw_r[l][k], (w_qkv_s, w_fc1_s)[k][l]
                    if k:
                        ins = nc.scalar.activation(s[32:32 + R + 1, :], r, ACT.Copy)
                    else:
                        for v, w in zip(by_part(r[:, 0:QK]), in_part(s[32:32 + R + 1, 0:QK])):
                            nc.scalar.activation(w, v, ACT.Copy)
                        ins = nc.scalar.activation(s[32:32 + R + 1, QK:], r[:, QK:], ACT.Copy)
                    ins.then_inc(high_w, 1)
                elif kind == "hT":
                    l, b, k, r, s = args
                    tok = tokens(s)
                    full(act, item)
                    released(act, ("acol", l, k))
                    m = (mod_r if r else mod)[l]
                    dst, n = (hT_r, R) if r else (hT, P)
                    nc.scalar.activation(dst[:, tok], bank_of(item)[0:n, tok], ACT.Identity, scale=m[:, k, SC, b:b + 1],
                                         bias=m[:, k, SH, b:b + 1]).then_inc(bank_free[BANK[item]], 1)
                elif kind == "qk":
                    l, b, c = args
                    full(act, item)
                    if QKN[item] > 3:
                        for which in range(2):
                            act.wait_ge(parts_out[which], 32 * ((QKN[item] - 1) // 3))
                    w = QKW[c]
                    nc.scalar.activation(parts[0:w, c, 0, :], bank_of(item)[0:w, :], ACT.Copy).then_inc(high_ready, 1)
                    if QKN[item] == 3:
                        act.wait_ge(rows_zero, 2)
                        nc.scalar.activation(QS[1][0:KROWS, :, :].bitcast(F32),
                                             zerosb[0:KROWS, None, :].to_broadcast([KROWS, H, T]).bitcast(F32),
                                             ACT.Copy).then_inc(q_zeroed[1], 1)
                elif kind == "mT":
                    g, = args
                    full(act, item)
                    if g >= 2:
                        act.wait_ge(m_in[g % 2], 16 * (g // 2))
                    nc.scalar.activation(mT[:, g % 2, :], bank_of(item).bitcast(BF16)[0:3 * HG, 0:T],
                                         ACT.Copy).then_inc(bank_free[BANK[item]], 1)
                elif kind == "scores":
                    g, u = args
                    kt, j = divmod(u, HG)
                    full(act, item)
                    if g * NT + kt >= 2:
                        attended(act, *divmod(g * NT + kt - 2, NT))
                    q0 = first_query(g // (B * NG), kt)
                    nc.scalar.activation(probs[:, kt % 2, j, q0:T], bank_of(item)[:, q0:T],
                                         ACT.Exp, scale=SCALE).then_inc(bank_free[BANK[item]], 1)
                elif kind == "oT":
                    g, = args
                    attended(act, g, NT - 1)
                    if g:
                        full(act, ("o", g - 1))
                    if g == 0:
                        act.wait_ge(low_w[2], 1)
                    nc.scalar.activation(OT[:, :], OB[:, :], ACT.Copy).then_inc(o_ready, 1)
                elif kind == "aT":
                    l, b, r, s = args
                    tok = tokens(s)
                    full(act, item)
                    if (l, b, r) == (0, 0, 1):
                        act.wait_ge(outputs_filled, 1)
                    dst, n = (aT_r, R) if r else (aT, P)
                    nc.scalar.activation(dst[0:n, tok], bank_of(item)[0:n, tok], ACT.Copy).then_inc(bank_free[BANK[item]], 1)
                elif kind == "fc1":
                    l, b, c, s = args
                    tok = tokens(s)
                    full(act, item)
                    last_use = ("gate", *before(l, b), c, 0)
                    if last_use in GATE:
                        act.wait_ge(g_ready, GATE[last_use])
                    if (l, b, c) == (0, 0, 0):
                        act.wait_ge(low_w[3], 1)
                        full(act, ("acol", 1, 1))
                        full(act, ("agate", 1, B - 1))
                    w = FW[c]
                    if l:
                        nc.scalar.activation(U[0:w, c, tok], bank_of(item)[0:w, tok], ACT.Tanh, scale=0.5)
                    else:
                        nc.scalar.activation(U[0:w, c, tok], bank_of(item)[0:w, tok], ACT.Square,
                                             scale=0.5 * (8 * GELU_C * GELU_A) ** 0.5)
                    nc.scalar.activation(xh[0:w, c, tok], bank_of(item)[0:w, tok], ACT.Copy,
                                         scale=0.5).then_inc(bank_free[BANK[item]], 1)
                elif kind == "tanh":
                    l, b, c, s = args
                    act.wait_ge(u_ready, GELU_U[("fc1", l, b, c, s)])
                    w = FW[c]
                    nc.scalar.activation(U[0:w, c, tokens(s)], U[0:w, c, tokens(s)], ACT.Tanh).then_inc(t_ready, 1)

        @block.vector
        def _(dve):
            chain = [0]

            def link(ins):
                chain[0] += 1
                ins.then_inc(dve_step, 1)
                dve.wait_ge(dve_step, chain[0])

            nc.vector.memset(cond_r[:, 3, :], 1.0)
            nc.vector.memset(w_qkv_s[0][:, :].bitcast(F32), 0.0).then_inc(filled_first, 1)
            dve.wait_ge(cond_in, 32)
            nc.vector.tensor_scalar(cond[:, 1, :], cond[:, 0, :], 0.5, None, ALU.mult)
            nc.vector.tensor_scalar(cond_r[0:R, 1, :], cond_r[0:R, 0, :], 0.5, None, ALU.mult).then_inc(silu_ready, 1)
            nc.vector.memset(hT_s[0:32, :].bitcast(F32), 1.0)
            nc.vector.memset(hT_s[32:64, :].bitcast(F32), 0.0)
            nc.vector.memset(hT_s[64:SR, :].bitcast(F32), 1.0)
            dve.wait_ge(th_ready, 1)
            dve.wait_ge(silu_ready, 1)
            nc.vector.scalar_tensor_tensor(cond[:, 3, :], cond[:, 2, :], 1.0, cond[:, 1, :], ALU.add, ALU.mult)
            nc.vector.scalar_tensor_tensor(cond_r[0:R, 3, :], cond_r[0:R, 2, :], 1.0, cond_r[0:R, 1, :],
                                           ALU.add, ALU.mult).then_inc(silu_ready, 1)
            def fill_late():
                dve.wait_ge(silu_ready, 2)
                for b in range(B):
                    nc.vector.tensor_copy(cond_w[:, b, :], cond[:, 3, b:b + 1].to_broadcast([P, P]))
                    ins = nc.vector.tensor_copy(cond_wr[:, b, :], cond_r[:, 3, b:b + 1].to_broadcast([R + 1, P]))
                ins.then_inc(wide_ready, 1)

                for b in range(B):
                    nc.vector.memset(V[b][:, :, :, D:VW], 1.0)
                nc.vector.memset(OB[:, :], 0.0)
                nc.vector.memset(aT_r[:, :], 1.0).then_inc(outputs_filled, 1)

            last_norm = None
            for item in ORDER["DVE"]:
                kind, *args = item
                bank = bank_of(item) if item in BANK else None
                if kind == "wsplit":
                    dve.wait_ge(high_w, 1)
                    low_values(nc.vector, 0, 0, lambda ins: None).then_inc(low_w[0], 1)
                elif kind == "acol":
                    l, k = args
                    full(dve, item)
                    for dst, n, at0 in ((mod[l], P, 0), (mod_r[l], R, 2 * B)):
                        nc.vector.tensor_copy(dst[:, k, SH, :], bank[0:n, at0:at0 + B])
                        ins = nc.vector.tensor_scalar(dst[:, k, SC, :], bank[0:n, at0 + B:at0 + 2 * B], 1.0, None, ALU.add)
                    ins.then_inc(bank_free[BANK[item]], 1)
                elif kind == "agate":
                    l, b = args
                    full(dve, item)
                    nc.vector.tensor_copy(gates[l][b][:, :, :], bank[:, 0:2 * C].rearrange("p (k c) -> p k c", k=2)
                                          ).then_inc(bank_free[BANK[item]], 1)
                elif kind == "stats":
                    l, b, k, s = args
                    t0, t1 = tiles(s)
                    if (l, k) == (0, 0):
                        dve.wait_ge(x_in[b], 16)
                    else:
                        for i in range(t0 // 2, t1 // 2):
                            released(dve, ("proj", l, b, i) if k else ("fc2", l - 1, b, i))
                    for t in range(t0, t1):
                        ins = nc.vector.bn_stats(stat[:, t, :], X[b][:, t, :])
                    link(ins)
                    for t in range(t0, t1):
                        ins = nc.vector.bn_aggr(mean[:, t, :], stat[:, t, :])
                    link(ins)
                    nc.vector.tensor_scalar(veps[:, t0:t1], mean[:, t0:t1, 1], EPS, None, ALU.add).then_inc(stats_ready, 1)
                elif kind == "norm":
                    l, b, k, s = args
                    dve.wait_ge(rstd_ready, STATS[("stats", l, b, k, s)])
                    dve.wait_ge(stats_ready, STATS[("stats", l, b, k, s)])
                    if last_norm and last_norm != (l, b, k):
                        for r in range(2):
                            full(dve, ("hT", *last_norm, r, 0))
                    last_norm = l, b, k
                    for t in range(*tiles(s)):
                        ins = nc.vector.tensor_scalar(hn[:, t, :], X[b][:, t, :], mean[:, t, 0:1],
                                                      rstd[:, t:t + 1], ALU.subtract, ALU.mult)
                    ins.then_inc(normed, 1)
                elif kind == "hT":
                    l, b, k, r, s = args
                    tok = tokens(s)
                    released(dve, item)
                    if r:
                        nc.vector.tensor_copy(hT_s[64:64 + R, tok], hT_r[:, tok])
                        link(nc.vector.tensor_copy(hT_s[0:R, tok], hT_r[:, tok]))
                        nc.vector.tensor_tensor(hT_s[32:32 + R, tok], hT_r[:, tok], hT_s[0:R, tok].bitcast(F32),
                                                ALU.subtract).then_inc(split, 1)
                    else:
                        link(nc.vector.tensor_copy(hT_p[0][:, tok], hT[:, tok]))
                        nc.vector.tensor_tensor(hT_p[1][:, tok], hT[:, tok], hT_p[0][:, tok].bitcast(F32),
                                                ALU.subtract).then_inc(split, 1)
                    if HTN[item] == 2:
                        fill_late()
                elif kind == "qk":
                    l, b, c = args
                    w = QKW[c]
                    dve.wait_ge(high_ready, QKN[item])
                    if QKN[item] > 1:
                        dve.wait_ge(parts_ready, QKN[item] - 1)
                    hi, mid, lo = (parts[0:w, c, i, :] for i in range(3))
                    nc.vector.tensor_tensor(rest[0:w, :], bank[0:w, :], hi, ALU.subtract).then_inc(bank_free[BANK[item]], 1)
                    released(dve, item)
                    link(nc.vector.tensor_copy(mid, rest[0:w, :]))
                    nc.vector.tensor_tensor(lo, rest[0:w, :], mid, ALU.subtract).then_inc(parts_ready, 1)
                elif kind == "v":
                    l, b, i = args
                    full(dve, item)
                    if l:
                        attended(dve, (b + 1) * NG - 1, NT - 1)
                    nc.vector.tensor_copy(V[b][:, 2 * i:2 * i + 2, :, 0:D],
                                          bank[:, 0:2 * C].rearrange("p (t h d) -> p t h d", t=2, h=H)
                                          ).then_inc(bank_free[BANK[item]], 1)
                elif kind == "max":
                    g, u = args
                    j, qt = divmod(u, NT)
                    full(dve, item)
                    if g >= 2 and u == 0:
                        dve.wait_ge(msplit_ready, g - 1)
                    nc.vector.tensor_reduce(negm[:, g % 2, qt, j:j + 1], bank[:, 0:keys_of(g // (B * NG), qt)],
                                            AX.X, ALU.max, negate=True).then_inc(bank_free[BANK[item]], 1)
                elif kind == "o":
                    g, = args
                    l, b, h = lb(g)
                    full(dve, item)
                    if l == 0 and g % NG == 0:
                        for i in ((1,) if b else (0, 2)):
                            dve.wait_ge(low_w[i], 1)
                    if l and g % NG == 0:
                        full(dve, ("aT", l - 1, b, 1, 0))
                    o = bank[:, :].rearrange("p (t j c) -> p t j c", t=NT, j=HG)
                    link(nc.vector.reciprocal(rden[:, :, :], o[:, :, :, D]))
                    nc.vector.tensor_tensor(at[b][:, :, h * D:(h + HG) * D].rearrange("p t (j d) -> p t j d", j=HG),
                                            o[:, :, :, 0:D], rden[:, :, :, None].to_broadcast([P, NT, HG, D]),
                                            ALU.mult).then_inc(bank_free[BANK[item]], 1)
                elif kind in ("proj", "fc2"):
                    l, b, i = args
                    full(dve, item)
                    x = X[b][:, 2 * i:2 * i + 2, :]
                    ins = nc.vector.tensor_tensor(x, x, bank[:, 0:2 * C].rearrange("p (t c) -> p t c", t=2), ALU.add)
                    ins.then_inc(bank_free[BANK[item]], 1)
                elif kind == "fc1":
                    l, b, c, s = args
                    w = FW[c]
                    released(dve, item)
                    u = U[0:w, c, tokens(s)]
                    nc.vector.scalar_tensor_tensor(u, u, 2 * GELU_C, xh[0:w, c, tokens(s)], ALU.add, ALU.mult).then_inc(u_ready, 1)
                elif kind == "gate":
                    l, b, c, s = args
                    w = FW[c]
                    if l == 0:
                        dve.wait_ge(t_ready, GELU_U[("fc1", l, b, c, s)])
                    released(dve, ("fc1", l, b, c, s))
                    u = U[0:w, c, tokens(s)]
                    nc.vector.scalar_tensor_tensor(u, u, 1.0, xh[0:w, c, tokens(s)], ALU.add, ALU.mult).then_inc(g_ready, 1)

        @block.tensor
        def _(pe):
            pe.wait_ge(consts, 2)

            def wide_product(bank, w, w_s, c0, n, s):
                cols, tok = slice(c0, c0 + n), tokens(s)
                o = bank[0:n, tok]
                nc.tensor.matmul(o, w[0][:, cols], hT_p[0][:, tok], start=True, stop=False)
                nc.tensor.matmul(o, w[0][:, cols], hT_p[1][:, tok], start=False, stop=False)
                nc.tensor.matmul(o, w[1][:, cols], hT_p[0][:, tok], start=False, stop=False)
                return nc.tensor.matmul(o, w_s[:, cols], hT_s[:, tok], start=False, stop=True)

            for item in ORDER["PE"]:
                kind, *args = item
                if item in BEFORE:
                    released(pe, BEFORE[item])
                bank = bank_of(item) if item in BANK else None
                filled_bank = bank_full[BANK[item]] if item in BANK else None
                if kind == "acol":
                    l, k = args
                    pe.wait_ge(silu_ready, 2)
                    pe.wait_ge(ada_in[l][0 if l else k], 48)
                    for r, n in enumerate((P, R)):
                        for s in range(2):
                            cols = slice((3 * k + s) * C + r * P, (3 * k + s) * C + r * P + n)
                            o = bank[0:n, (2 * r + s) * B:(2 * r + s + 1) * B]
                            nc.tensor.matmul(o, w_ada[l][:, cols], cond[:, 3, :], start=True, stop=False)
                            ins = nc.tensor.matmul(o, w_ada_r[l][:, cols], cond_r[:, 3, :], start=False, stop=True)
                    ins.then_inc(filled_bank, 1)
                elif kind == "agate":
                    l, b = args
                    pe.wait_ge(wide_ready, 1)
                    for k in range(2):
                        pe.wait_ge(ada_in[l][0 if l else k], 48)
                        c0 = (3 * k + GA) * C
                        o = bank[:, k * C:(k + 1) * C]
                        nc.tensor.matmul(o, cond_w[:, b, :], w_ada[l][:, c0:c0 + C], start=True, stop=False)
                        ins = nc.tensor.matmul(o, cond_wr[:, b, :], w_ada_r[l][:, c0:c0 + C], start=False, stop=True)
                    ins.then_inc(filled_bank, 1)
                elif kind == "hT":
                    l, b, k, r, s = args
                    pe.wait_ge(normed, NORM[("norm", l, b, k, s)])
                    for t in range(*tiles(s)):
                        src = hn[:, t, P:C] if r else hn[:, t, 0:P]
                        n = R if r else P
                        ins = nc.tensor.transpose(bank[0:n, t * P:(t + 1) * P], src, ident[:, :])
                    ins.then_inc(filled_bank, 1)
                elif kind == "qk":
                    l, b, c = args
                    pe.wait_ge(split, HTN[("hT", l, b, 0, 0, 0)])
                    pe.wait_ge(low_w[2 * l], 1)
                    wide_product(bank, w_qk[l], w_qkv_s[l], c * P, QKW[c], 0).then_inc(filled_bank, 1)
                elif kind == "v":
                    l, b, i = args
                    for t in range(2):
                        tok = slice((2 * i + t) * P, (2 * i + t + 1) * P)
                        o = bank[:, t * C:(t + 1) * C]
                        nc.tensor.matmul(o, hT[:, tok], w_v[l][:, :], start=True, stop=False)
                        ins = nc.tensor.matmul(o, hT_s[:, tok], w_qkv_s[l][:, QK:3 * C], start=False, stop=True)
                    ins.then_inc(filled_bank, 1)
                elif kind == "max":
                    g, u = args
                    l, b, h = lb(g)
                    j, qt = divmod(u, NT)
                    if u == 0 and g % NG < 2:
                        pe.wait_ge(stacked[g // NG][g % NG], 16 * (NSTACK + (g % NG == 0)))
                    w = keys_of(l, qt)
                    o = bank
                    q = QS[b][0:KROWS, h + j, qt * P:(qt + 1) * P]
                    ins = nc.tensor.matmul(o[:, 0:w], q, KS[b][0:KROWS, h + j, 0:w], start=True, stop=(l == 0))
                    if l:
                        ins = nc.tensor.matmul(o[:, w - P:w], identb[:, :], mask_qk[:, :], start=False, stop=True)
                    ins.then_inc(filled_bank, 1)
                elif kind == "mT":
                    g, = args
                    pe.wait_ge(msplit_ready, g + 1)
                    for t in range(NT):
                        ins = nc.tensor.transpose(bank.bitcast(BF16)[0:3 * HG, t * P:(t + 1) * P],
                                                  msp[:, t, :, :].rearrange("p s j -> p (s j)"), identb[:, :])
                    ins.then_inc(filled_bank, 1)
                elif kind == "scores":
                    g, u = args
                    l, b, h = lb(g)
                    kt, j = divmod(u, HG)
                    if u == 0:
                        pe.wait_ge(m_in[g % 2], 16 * (g // 2 + 1))
                    q0 = first_query(l, kt)
                    ins = nc.tensor.matmul(bank[:, q0:T], KS[b][0:KROWS, h + j, kt * P:(kt + 1) * P],
                                           QS[b][0:KROWS, h + j, q0:T], start=True, stop=(l == 0))
                    if l:
                        ins = nc.tensor.matmul(bank[:, q0:q0 + P], identb[:, :], mask_kq[:, :], start=False, stop=True)
                    ins.then_inc(filled_bank, 1)
                elif kind == "pv":
                    g, kt = args
                    l, b, h = lb(g)
                    released(pe, ("scores", g, kt * HG + HG - 1))
                    if kt == 0 and g:
                        pe.wait_ge(o_ready, g)
                    if g == 0 and kt == 0:
                        pe.wait_ge(outputs_filled, 1)
                    if kt == 0 and g % NG == 0:
                        for i in range(2):
                            released(pe, ("v", l, b, i))
                    q0 = first_query(l, kt)
                    for j in range(HG):
                        ins = nc.tensor.matmul(OB[CT * j:CT * j + VW, q0:T], V[b][:, kt, h + j, :],
                                               probs[:, kt % 2, j, q0:T], start=(kt == 0), stop=(kt == NT - 1))
                    ins.then_inc(pv_done, 1)
                elif kind == "o":
                    g, = args
                    pe.wait_ge(o_ready, g + 1)
                    for t in range(NT):
                        ins = nc.tensor.transpose(bank[:, t * P:(t + 1) * P], OT[:, t * P:(t + 1) * P], ident[:, :])
                    ins.then_inc(filled_bank, 1)
                elif kind == "aT":
                    l, b, r, s = args
                    released(pe, ("o", (l * B + b + 1) * NG - 1))
                    for t in range(*tiles(s)):
                        src = at[b][:, t, P:C] if r else at[b][:, t, 0:P]
                        n = R if r else P
                        ins = nc.tensor.transpose(bank[0:n, t * P:(t + 1) * P], src, ident[:, :])
                    ins.then_inc(filled_bank, 1)
                elif kind == "proj":
                    l, b, i = args
                    pe.wait_ge(gated, l * B + b + 1)
                    for r in range(2):
                        released(pe, ("aT", l, b, r, part_with(l, b, i)))
                    for t in range(2):
                        tok = slice((2 * i + t) * P, (2 * i + t + 1) * P)
                        o = bank[:, t * C:(t + 1) * C]
                        nc.tensor.matmul(o, aT[:, tok], g_proj[l][b][:, :], start=True, stop=False)
                        ins = nc.tensor.matmul(o, aT_r[:, tok], g_proj_r[l][b][:, :], start=False, stop=True)
                    ins.then_inc(filled_bank, 1)
                elif kind == "fc1":
                    l, b, c, s = args
                    pe.wait_ge(split, HTN[("hT", l, b, 1, 0, s)])
                    pe.wait_ge(low_w[2 * l + 1], 1)
                    wide_product(bank, w_fc1[l], w_fc1_s[l], c * P, FW[c], s).then_inc(filled_bank, 1)
                elif kind == "fc2":
                    l, b, i = args
                    pe.wait_ge(filled_late, 1)
                    for t in range(2):
                        tok = slice((2 * i + t) * P, (2 * i + t + 1) * P)
                        for c in range(NF):
                            if t == 0:
                                pe.wait_ge(g_ready, GATE[("gate", l, b, c, part_with(l, b, i))])
                            w = SR if c == NF - 1 else P
                            ins = nc.tensor.matmul(bank[:, t * C:(t + 1) * C], U[0:w, c, tok], g_fc2[l][b][0:w, c, :],
                                                   start=(c == 0), stop=(c == NF - 1))
                    ins.then_inc(filled_bank, 1)


def kernel(**inputs):
    import numpy as np
    from concourse import bacc
    from concourse.bass_utils import run_bass_kernel_spmd

    nc = bacc.Bacc("TRN2", target_bir_lowering=False, num_devices=1)
    arrays, aps = {}, {}
    for name, value in inputs.items():
        v = np.ascontiguousarray(np.asarray(value).T if name == "cond_1152" else value)
        arrays["in_" + name] = v
        aps[name] = nc.dram_tensor("in_" + name, v.shape, mybir.dt.from_np(v.dtype), kind="ExternalInput").ap()
    out = nc.dram_tensor("out", (B, T, C), F32, kind="ExternalOutput").ap()
    two_block_kernel(nc, aps, out)
    r = run_bass_kernel_spmd(nc, [arrays], core_ids=[0])
    return r.results[0]["out"]
```
